# Optimizing a Trainium2 kernel written in Bass

```python
import numpy as np
import jax
import jax.numpy as jnp

def _softmax(x, axis=-1):
    return jax.nn.softmax(x, axis=axis)

def _gelu(x):
    return jax.nn.gelu(x, approximate=True)

def _silu(x):
    return jax.nn.silu(x)

def _sigmoid(x):
    return jax.nn.sigmoid(x)

def _layernorm(x, axis=-1, eps=1e-05):
    m = jnp.mean(x, axis=axis, keepdims=True)
    v = jnp.var(x, axis=axis, keepdims=True)
    return (x - m) / jnp.sqrt(v + eps)

def _scatter_add(tgt, idx, src, axis=0):
    return tgt.at[idx].add(src)

def _segment_sum(src, seg, n):
    return jax.ops.segment_sum(src, seg, n)
kernel_name = 'mk_adj_resnorm_d4_adj_r2_e0824b'

def setup_inputs(seed: int=0):
    np.random.seed(seed)
    _w = jnp.asarray

    def _rec_inputs():
        import jax
        import jax.numpy as jnp
        _gk = jax.random.key(seed)
        x = -0.0002928 + 1 * jax.random.normal(jax.random.fold_in(_gk, 1), (128, 128, 256), jnp.float32)
        _a = jax.random.bernoulli(jax.random.fold_in(_gk, 2), 0.125, (128, 128, 128))
        _a = jnp.logical_or(_a, jnp.swapaxes(_a, -1, -2))
        _a = jnp.logical_or(_a, jnp.eye(128, dtype=bool))
        adj = _a
        return (x, adj)
    x, adj = _rec_inputs()

    def _L0_gnn_setup():
        import jax, jax.numpy as jnp
        import numpy as np
        QUERY_DIM = 256
        HEADS = 4
        DIM_HEAD = 64
        INNER = HEADS * DIM_HEAD
        B, N = (4, 1024)
        key = jax.random.key(seed)
        ks = jax.random.split(key, 6)
        s = 1.0 / np.sqrt(QUERY_DIM)
        x = jax.random.normal(ks[0], (B, N, QUERY_DIM), dtype=jnp.float32)
        adjacency_mask = jax.random.randint(ks[1], (B, N, N), 0, 2) > 0
        Wq = jax.random.normal(ks[2], (QUERY_DIM, INNER), dtype=jnp.float32) * s
        Wk = jax.random.normal(ks[3], (QUERY_DIM, INNER), dtype=jnp.float32) * s
        Wv = jax.random.normal(ks[4], (QUERY_DIM, INNER), dtype=jnp.float32) * s
        Wo = jax.random.normal(ks[5], (INNER, QUERY_DIM), dtype=jnp.float32) * (1.0 / np.sqrt(INNER))
        bo = jnp.zeros((QUERY_DIM,), dtype=jnp.float32)
        return {'x': x, 'adjacency_mask': adjacency_mask, 'Wq': Wq, 'Wk': Wk, 'Wv': Wv, 'Wo': Wo, 'bo': bo}
    _L0_gnn_all = _L0_gnn_setup()
    _L0_gnn_in = {k: v for k, v in _L0_gnn_all.items() if k in ('Wq', 'Wk', 'Wv', 'Wo', 'bo')}
    del _L0_gnn_all

    def _L1_gnn_setup():
        import jax, jax.numpy as jnp
        import numpy as np
        QUERY_DIM = 256
        HEADS = 4
        DIM_HEAD = 64
        INNER = HEADS * DIM_HEAD
        B, N = (4, 1024)
        key = jax.random.key(seed)
        ks = jax.random.split(key, 6)
        s = 1.0 / np.sqrt(QUERY_DIM)
        x = jax.random.normal(ks[0], (B, N, QUERY_DIM), dtype=jnp.float32)
        adjacency_mask = jax.random.randint(ks[1], (B, N, N), 0, 2) > 0
        Wq = jax.random.normal(ks[2], (QUERY_DIM, INNER), dtype=jnp.float32) * s
        Wk = jax.random.normal(ks[3], (QUERY_DIM, INNER), dtype=jnp.float32) * s
        Wv = jax.random.normal(ks[4], (QUERY_DIM, INNER), dtype=jnp.float32) * s
        Wo = jax.random.normal(ks[5], (INNER, QUERY_DIM), dtype=jnp.float32) * (1.0 / np.sqrt(INNER))
        bo = jnp.zeros((QUERY_DIM,), dtype=jnp.float32)
        return {'x': x, 'adjacency_mask': adjacency_mask, 'Wq': Wq, 'Wk': Wk, 'Wv': Wv, 'Wo': Wo, 'bo': bo}
    _L1_gnn_all = _L1_gnn_setup()
    _L1_gnn_in = {k: v for k, v in _L1_gnn_all.items() if k in ('Wq', 'Wk', 'Wv', 'Wo', 'bo')}
    del _L1_gnn_all

    def _L2_gnn_setup():
        import jax, jax.numpy as jnp
        import numpy as np
        QUERY_DIM = 256
        HEADS = 4
        DIM_HEAD = 64
        INNER = HEADS * DIM_HEAD
        B, N = (4, 1024)
        key = jax.random.key(seed)
        ks = jax.random.split(key, 6)
        s = 1.0 / np.sqrt(QUERY_DIM)
        x = jax.random.normal(ks[0], (B, N, QUERY_DIM), dtype=jnp.float32)
        adjacency_mask = jax.random.randint(ks[1], (B, N, N), 0, 2) > 0
        Wq = jax.random.normal(ks[2], (QUERY_DIM, INNER), dtype=jnp.float32) * s
        Wk = jax.random.normal(ks[3], (QUERY_DIM, INNER), dtype=jnp.float32) * s
        Wv = jax.random.normal(ks[4], (QUERY_DIM, INNER), dtype=jnp.float32) * s
        Wo = jax.random.normal(ks[5], (INNER, QUERY_DIM), dtype=jnp.float32) * (1.0 / np.sqrt(INNER))
        bo = jnp.zeros((QUERY_DIM,), dtype=jnp.float32)
        return {'x': x, 'adjacency_mask': adjacency_mask, 'Wq': Wq, 'Wk': Wk, 'Wv': Wv, 'Wo': Wo, 'bo': bo}
    _L2_gnn_all = _L2_gnn_setup()
    _L2_gnn_in = {k: v for k, v in _L2_gnn_all.items() if k in ('Wq', 'Wk', 'Wv', 'Wo', 'bo')}
    del _L2_gnn_all

    def _L3_gnn_setup():
        import jax, jax.numpy as jnp
        import numpy as np
        HEAD_NUM = 8
        THRESHOLD = 0.1
        NEG = -10000000000.0
        COS_EPS = 1e-08
        B, S, D = (8, 512, 256)
        D_OUT = 256
        key = jax.random.key(seed)
        ks = jax.random.split(key, 12)
        embs = jax.random.normal(ks[0], (B, S, D), dtype=jnp.float32)
        lengths = jax.random.randint(ks[1], (B,), S // 2, S + 1)
        pad = jnp.arange(S)[None, :] >= lengths[:, None]
        score_mask = pad[:, :, None] | pad[:, None, :]
        sc = 1.0 / np.sqrt(D)
        mk = lambda k, shp: jax.random.normal(k, shp, dtype=jnp.float32) * sc
        return {'embs': embs, 'score_mask': score_mask, 'map_w': mk(ks[2], (D, D)), 'map_b': jnp.zeros((D,), jnp.float32), 'q_w': mk(ks[3], (D, D)), 'q_b': jnp.zeros((D,), jnp.float32), 'k_w': mk(ks[4], (D, D)), 'k_b': jnp.zeros((D,), jnp.float32), 'gcn_map_w': mk(ks[5], (D_OUT, D)), 'gcn_map_b': jnp.zeros((D_OUT,), jnp.float32), 'gcn_W': jax.random.normal(ks[6], (D_OUT // HEAD_NUM, D_OUT // HEAD_NUM), dtype=jnp.float32) * (1.0 / np.sqrt(D_OUT // HEAD_NUM))}
    _L3_gnn_all = _L3_gnn_setup()
    _L3_gnn_in = {k: v for k, v in _L3_gnn_all.items() if k in ('map_w', 'map_b', 'q_w', 'q_b', 'k_w', 'k_b', 'gcn_map_w', 'gcn_map_b', 'gcn_W')}
    del _L3_gnn_all
    return {'x': x, 'adj': adj, 'L0_gnn_Wq': _L0_gnn_in['Wq'], 'L0_gnn_Wk': _L0_gnn_in['Wk'], 'L0_gnn_Wv': _L0_gnn_in['Wv'], 'L0_gnn_Wo': _L0_gnn_in['Wo'], 'L0_gnn_bo': _L0_gnn_in['bo'], 'L1_gnn_Wq': _L1_gnn_in['Wq'], 'L1_gnn_Wk': _L1_gnn_in['Wk'], 'L1_gnn_Wv': _L1_gnn_in['Wv'], 'L1_gnn_Wo': _L1_gnn_in['Wo'], 'L1_gnn_bo': _L1_gnn_in['bo'], 'L2_gnn_Wq': _L2_gnn_in['Wq'], 'L2_gnn_Wk': _L2_gnn_in['Wk'], 'L2_gnn_Wv': _L2_gnn_in['Wv'], 'L2_gnn_Wo': _L2_gnn_in['Wo'], 'L2_gnn_bo': _L2_gnn_in['bo'], 'L3_gnn_map_w': _L3_gnn_in['map_w'], 'L3_gnn_map_b': _L3_gnn_in['map_b'], 'L3_gnn_q_w': _L3_gnn_in['q_w'], 'L3_gnn_q_b': _L3_gnn_in['q_b'], 'L3_gnn_k_w': _L3_gnn_in['k_w'], 'L3_gnn_k_b': _L3_gnn_in['k_b'], 'L3_gnn_gcn_map_w': _L3_gnn_in['gcn_map_w'], 'L3_gnn_gcn_map_b': _L3_gnn_in['gcn_map_b'], 'L3_gnn_gcn_W': _L3_gnn_in['gcn_W']}

def reference(x, adj, L0_gnn_Wq, L0_gnn_Wk, L0_gnn_Wv, L0_gnn_Wo, L0_gnn_bo, L1_gnn_Wq, L1_gnn_Wk, L1_gnn_Wv, L1_gnn_Wo, L1_gnn_bo, L2_gnn_Wq, L2_gnn_Wk, L2_gnn_Wv, L2_gnn_Wo, L2_gnn_bo, L3_gnn_map_w, L3_gnn_map_b, L3_gnn_q_w, L3_gnn_q_b, L3_gnn_k_w, L3_gnn_k_b, L3_gnn_gcn_map_w, L3_gnn_gcn_map_b, L3_gnn_gcn_W):
    import jax
    import jax.numpy as jnp

    def _L0_gnn_ref(x, adjacency_mask, Wq, Wk, Wv, Wo, bo):
        import jax, jax.numpy as jnp
        import numpy as np
        QUERY_DIM = 256
        HEADS = 4
        DIM_HEAD = 64
        INNER = HEADS * DIM_HEAD
        B, N = (4, 1024)
        scale = DIM_HEAD ** (-0.5)

        def split_heads(t):
            b, n, _ = t.shape
            return t.reshape(b, n, HEADS, DIM_HEAD).transpose(0, 2, 1, 3)
        q = split_heads(x @ Wq)
        k = split_heads(x @ Wk)
        v = split_heads(x @ Wv)
        sim = jnp.einsum('bhid,bhjd->bhij', q, k) * scale
        neg = -jnp.finfo(sim.dtype).max
        sim = jnp.where(adjacency_mask[:, None, :, :], sim, neg)
        attn = jax.nn.softmax(sim, axis=-1)
        out = jnp.einsum('bhij,bhjd->bhid', attn, v)
        out = out.transpose(0, 2, 1, 3).reshape(x.shape[0], x.shape[1], INNER)
        return out @ Wo + bo

    def _L1_gnn_ref(x, adjacency_mask, Wq, Wk, Wv, Wo, bo):
        import jax, jax.numpy as jnp
        import numpy as np
        QUERY_DIM = 256
        HEADS = 4
        DIM_HEAD = 64
        INNER = HEADS * DIM_HEAD
        B, N = (4, 1024)
        scale = DIM_HEAD ** (-0.5)

        def split_heads(t):
            b, n, _ = t.shape
            return t.reshape(b, n, HEADS, DIM_HEAD).transpose(0, 2, 1, 3)
        q = split_heads(x @ Wq)
        k = split_heads(x @ Wk)
        v = split_heads(x @ Wv)
        sim = jnp.einsum('bhid,bhjd->bhij', q, k) * scale
        neg = -jnp.finfo(sim.dtype).max
        sim = jnp.where(adjacency_mask[:, None, :, :], sim, neg)
        attn = jax.nn.softmax(sim, axis=-1)
        out = jnp.einsum('bhij,bhjd->bhid', attn, v)
        out = out.transpose(0, 2, 1, 3).reshape(x.shape[0], x.shape[1], INNER)
        return out @ Wo + bo

    def _L2_gnn_ref(x, adjacency_mask, Wq, Wk, Wv, Wo, bo):
        import jax, jax.numpy as jnp
        import numpy as np
        QUERY_DIM = 256
        HEADS = 4
        DIM_HEAD = 64
        INNER = HEADS * DIM_HEAD
        B, N = (4, 1024)
        scale = DIM_HEAD ** (-0.5)

        def split_heads(t):
            b, n, _ = t.shape
            return t.reshape(b, n, HEADS, DIM_HEAD).transpose(0, 2, 1, 3)
        q = split_heads(x @ Wq)
        k = split_heads(x @ Wk)
        v = split_heads(x @ Wv)
        sim = jnp.einsum('bhid,bhjd->bhij', q, k) * scale
        neg = -jnp.finfo(sim.dtype).max
        sim = jnp.where(adjacency_mask[:, None, :, :], sim, neg)
        attn = jax.nn.softmax(sim, axis=-1)
        out = jnp.einsum('bhij,bhjd->bhid', attn, v)
        out = out.transpose(0, 2, 1, 3).reshape(x.shape[0], x.shape[1], INNER)
        return out @ Wo + bo

    def _L3_gnn_ref(embs, score_mask, map_w, map_b, q_w, q_b, k_w, k_b, gcn_map_w, gcn_map_b, gcn_W):
        import jax, jax.numpy as jnp
        import numpy as np
        HEAD_NUM = 8
        THRESHOLD = 0.1
        NEG = -10000000000.0
        COS_EPS = 1e-08
        B, S, D = (8, 512, 256)
        D_OUT = 256
        b, s, d = embs.shape
        h, dk = (HEAD_NUM, d // HEAD_NUM)
        sm = score_mask[:, None, :, :]
        keep = (~sm[..., 0:1]).astype(embs.dtype)
        m = embs @ map_w.T + map_b
        sem = m.reshape(b, s, h, dk).transpose(0, 2, 1, 3)
        norm = jnp.maximum(jnp.linalg.norm(sem, axis=-1, keepdims=True), COS_EPS)
        n = sem / norm
        cos = jnp.einsum('bhsd,bhtd->bhst', n, n)
        cos = cos * (~sm).astype(cos.dtype)
        cos_adj = (cos > THRESHOLD).astype(embs.dtype)
        q = (m @ q_w.T + q_b).reshape(b, s, h, dk).transpose(0, 2, 1, 3)
        k = (m @ k_w.T + k_b).reshape(b, s, h, dk).transpose(0, 2, 1, 3)
        scores = jnp.einsum('bhsd,bhtd->bhst', q, k) / jnp.sqrt(jnp.asarray(dk, embs.dtype))
        scores = jnp.where(sm, NEG, scores)
        p_attn = jax.nn.softmax(scores, axis=-1) * keep
        adj = cos_adj * p_attn
        hk = gcn_map_w.shape[0] // h
        sem_h = (embs @ gcn_map_w.T + gcn_map_b).reshape(b, s, h, hk).transpose(2, 0, 1, 3)
        adj_h = adj.transpose(1, 0, 2, 3)
        Ax = jnp.einsum('hbst,hbtd->hbsd', adj_h, sem_h)
        AxW = Ax @ gcn_W.T
        denom = adj_h.sum(-1, keepdims=True) + 1.0
        out = jax.nn.relu(AxW / denom)
        out = out.transpose(1, 2, 0, 3).reshape(b, s, h * hk)
        return out
    x = _layernorm(x + _L0_gnn_ref(x, adj, L0_gnn_Wq, L0_gnn_Wk, L0_gnn_Wv, L0_gnn_Wo, L0_gnn_bo), axis=-1)
    x = _layernorm(x + _L1_gnn_ref(x, adj, L1_gnn_Wq, L1_gnn_Wk, L1_gnn_Wv, L1_gnn_Wo, L1_gnn_bo), axis=-1)
    x = _layernorm(x + _L2_gnn_ref(x, adj, L2_gnn_Wq, L2_gnn_Wk, L2_gnn_Wv, L2_gnn_Wo, L2_gnn_bo), axis=-1)
    x = _layernorm(x + _L3_gnn_ref(x, adj, L3_gnn_map_w, L3_gnn_map_b, L3_gnn_q_w, L3_gnn_q_b, L3_gnn_k_w, L3_gnn_k_b, L3_gnn_gcn_map_w, L3_gnn_gcn_map_b, L3_gnn_gcn_W), axis=-1)
    return x

_drawn_inputs = setup_inputs


def setup_inputs(seed=0):
    import zlib

    import numpy as np

    out = dict(_drawn_inputs(seed))
    spreads = {'L0_gnn_bo': (0.0, 0.1),
     'L1_gnn_bo': (0.0, 0.1),
     'L2_gnn_bo': (0.0, 0.1),
     'L3_gnn_map_b': (0.0, 0.531),
     'L3_gnn_q_b': (0.0, 0.8),
     'L3_gnn_k_b': (0.0, 0.8),
     'L3_gnn_gcn_map_b': (0.0, 0.375)}
    factors = {}
    for name, (base, spread) in spreads.items():
        noise = np.random.default_rng([zlib.crc32(name.encode()), seed]).standard_normal(out[name].shape)
        drawn = base * np.exp(spread * noise) if base else spread * noise
        out[name] = jnp.asarray(drawn.astype(out[name].dtype))
    for name, factor in factors.items():
        out[name] = (out[name] * factor).astype(out[name].dtype)
    return out
```

```python
from contextlib import ExitStack

import concourse.bass as bass
from concourse import mybir

F32 = mybir.dt.float32
F32R = mybir.dt.float32r
BF16 = mybir.dt.bfloat16
U8 = mybir.dt.uint8
I32 = mybir.dt.int32
ALU = mybir.AluOpType
ACT = mybir.ActivationFunctionType
AX_X = mybir.AxisListType.X

P = 128
STREAMS = 2
GB = 2
MASKED = 2.0 ** 100
LN_EPS = 1e-5

HI, LO = 0, 1
SPLIT_PRODUCTS = [(HI, HI), (HI, LO), (LO, HI)]


def build(nc, x, adj, attn_w, attn_bo, gcn_w, gcn_cols, gcn_tail, out):
    B, N, D = x.shape
    LAYERS = attn_w.shape[0]
    H, DH = 4, 64
    GH, DK = 8, 32
    DC = D // P
    NT = B // (GB * STREAMS)
    GF = GB * D
    THRESHOLD = 0.1
    GSCALE = float(DK) ** -0.5
    NORM2_MIN = 1e-16
    assert N == P and DC == 2 and H * DH == D and GH * DK == D
    WQ, WK, WV, WO = range(4)
    WM, WMQ, WMK, WG = range(4)
    RAW_MT, RAW_M, RAW_QT, RAW_KT = range(4)

    with ExitStack() as ctx:
        def sb(name, shape, dt=F32):
            return ctx.enter_context(nc.sbuf_tensor(name, shape, dt))

        def sem(name):
            return ctx.enter_context(nc.semaphore(name))

        def sems(name):
            return [sem(f"{name}{s}") for s in range(STREAMS)]

        w_part = [sb("w_hi", [P, 4, DC, D], F32R), sb("w_lo", [P, 4, DC, D], F32R)]
        bias_rows = sb("bias_rows", [P, D])
        ident = sb("ident", [P, P])
        ident_bf = sb("ident_bf", [P, P], BF16)
        head_ones = sb("head_ones", [P, P])
        tail_w = sb("tail_w", [P, P])
        cols = sb("cols", [P, 4, DC])
        fused_b = sb("fused_b", [P, 2, DC])
        gb_wide = sb("gb_wide", [P, DC, P])
        eps_col = sb("eps_col", [P, 1])

        def per_stream(name, shape, dt=F32):
            return [sb(f"{name}{s}", shape, dt) for s in range(STREAMS)]

        stage = per_stream("stage", [P, GB, D])
        x_keep = per_stream("x_keep", [P, GF])
        x_new = per_stream("x_new", [P, GF])
        xt = [[sb(f"xt_hi{s}", [P, DC, GB * N], F32R), sb(f"xt_lo{s}", [P, DC, GB * N], F32R)]
              for s in range(STREAMS)]
        ot = [[sb(f"ot_hi{s}", [P, DC, GB * N], F32R), sb(f"ot_lo{s}", [P, DC, GB * N], F32R)]
              for s in range(STREAMS)]
        qt = per_stream("qt", [P, DC, GB * N])
        kt = per_stream("kt", [P, DC, GB * N])
        v_buf = per_stream("v_buf", [P, GB * GH * (DK + 1)])
        probs_all = sb("probs_all", [P, STREAMS, GB * H * N])
        probs_t_all = sb("probs_t_all", [P, STREAMS, GB * H * N])
        k_part = per_stream("k_part", [P, 2, DC, GB, N], F32R)
        n_part = per_stream("n_part", [P, 2, DC, GB, N], F32R)
        k_diag = per_stream("k_diag", [P, 4, 2, DC, GB, N], F32R)
        n_diag = per_stream("n_diag", [P, 4, 2, DC, GB, N], F32R)
        mask_words = per_stream("mask_words", [P, GB, N // 4], I32)
        mask_raw = [mask_words[s][:].bitcast(U8) for s in range(STREAMS)]
        mask_add = per_stream("mask_add", [P, GB, N], BF16)
        neg_max = per_stream("neg_max", [P, 8])
        row_sum = per_stream("row_sum", [P, GB, GH])
        half_out = per_stream("half_out", [P, GB * 4 * (DK + 1)])
        rcp = per_stream("rcp", [P, GB * GH])
        total = per_stream("total", [P, GB * GH])
        keep = per_stream("keep", [P, GB, 1])
        bn = per_stream("bn", [P, GB, 6])
        mean_var = per_stream("mean_var", [P, GB, 2])
        log_var = per_stream("log_var", [P, GB])
        rstd = per_stream("rstd", [P, GB])

        raw_w = probs_all[:].rearrange("p s (m c o) -> p (s m) c o", m=2, c=DC)
        raw_g = probs_t_all[:, 0, 0:DC * D].rearrange("p (c o) -> p c o", c=DC)
        probs = [probs_all[:, s].rearrange("p (b h j) -> p b h j", b=GB, h=H) for s in range(STREAMS)]
        probs_t = [probs_t_all[:, s].rearrange("p (b h i) -> p b h i", b=GB, h=H) for s in range(STREAMS)]
        attn_out = [probs_all[:, s, 0:GF].rearrange("p (b f) -> p b f", b=GB) for s in range(STREAMS)]
        y_sum = [probs_t_all[:, s, 0:GF] for s in range(STREAMS)]
        v_ones = [v_buf[s][:, 0:GB * H * (DH + 1)].rearrange("p (b h d) -> p b h d", b=GB, h=H)
                  for s in range(STREAMS)]
        g_ones = [v_buf[s][:].rearrange("p (b h d) -> p b h d", b=GB, h=GH) for s in range(STREAMS)]
        flat = {name: [v[s][:].rearrange("p c n -> p (c n)") for s in range(STREAMS)]
                for name, v in (("m", qt), ("sq", kt))}

        psum = [ctx.enter_context(nc.psum_tensor(f"psum{s}", [P, 4, 512], F32)) for s in range(STREAMS)]
        SC0, SC1, WK0, WK1 = range(4)

        x_mid = nc.dram_tensor("x_mid", [B, N, D], F32, kind="Internal").ap()

        FREED, FULL = 1, 2
        loaded = sems("loaded")
        mask_loaded = sems("mask_loaded")
        kept = sems("kept")
        stored = sems("stored")
        const_ready = sem("const_ready")
        ones_ready = sem("ones_ready")
        raw_loaded = sem("raw_loaded")
        w_hi_ready = sem("w_hi_ready")
        w_split = sem("w_split")
        mask_ready = sems("mask_ready")
        x_keep_ready = sems("x_keep_ready")
        xt_psum = sems("xt_psum")
        xt_hi_ready, xt_lo_ready = sems("xt_hi_ready"), sems("xt_lo_ready")
        q_psum, k_psum, v_psum = sems("q_psum"), sems("k_psum"), sems("v_psum")
        q_ready, k_ready, v_ready = sems("q_ready"), sems("k_ready"), sems("v_ready")
        scores_psum = sems("scores_psum")
        max_ready = sems("max_ready")
        probs_ready = sems("probs_ready")
        pt_psum = sems("pt_psum")
        pt0_ready, pt1_ready = sems("pt0_ready"), sems("pt1_ready")
        o_psum = sems("o_psum")
        rcp_ready = sems("rcp_ready")
        o_ready = sems("o_ready")
        ot_psum = sems("ot_psum")
        ot_hi_ready, ot_lo_ready = sems("ot_hi_ready"), sems("ot_lo_ready")
        wo_psum = sems("wo_psum")
        y_ready = sems("y_ready")
        bn_ready, mv_ready = sems("bn_ready"), sems("mv_ready")
        log_ready, rstd_ready = sems("log_ready"), sems("rstd_ready")
        x_done = sems("x_done")
        graph_raw_loaded = sem("graph_raw_loaded")
        gb_wide_ready = sem("gb_wide_ready")
        fused_psum, fused_hi_ready, fused_ready = sem("fused_psum"), sem("fused_hi_ready"), sem("fused_ready")
        keep_ready = sems("keep_ready")
        m_psum, m_ready, sq_ready = sems("m_psum"), sems("m_ready"), sems("sq_ready")
        ss_psum, ss_ready, ss_log_ready = sems("ss_psum"), sems("ss_ready"), sems("ss_log_ready")
        inv_norm_ready, n_ready = sems("inv_norm_ready"), sems("n_ready")
        q_hi_ready, q_lo_ready = sems("q_hi_ready"), sems("q_lo_ready")
        k_hi_ready, k_lo_ready = sems("k_hi_ready"), sems("k_lo_ready")
        n_hi_ready, n_lo_ready = sems("n_hi_ready"), sems("n_lo_ready")
        k_spread, n_spread = sems("k_spread"), sems("n_spread")
        g_scores_psum, g_cos_psum = sems("g_scores_psum"), sems("g_cos_psum")
        g_max_ready = [sems(f"g_max{b}_ready") for b in range(GB)]
        g_exp_ready = [sems(f"g_exp{b}_ready") for b in range(GB)]
        gate_ready = [sems(f"gate{b}_ready") for b in range(GB)]
        gt_psum = sems("gt_psum")
        gt_ready = [sems(f"gt{b}_ready") for b in range(GB)]
        g_out_psum = sems("g_out_psum")
        half_ready = sems("half_ready")
        total_ready = sems("total_ready")
        g_rcp_ready, g_scale_ready = sems("g_rcp_ready"), sems("g_scale_ready")
        scaled_ready = sems("scaled_ready")

        ATTN_ITS = LAYERS * NT

        block = ctx.enter_context(nc.Block())

        def graphs(t, s):
            return bass.ds(t * (STREAMS * GB) + s * GB, GB)

        def credit(eng, *families):
            for family in families:
                for one in family:
                    eng.sem_inc(one, 1)

        @block.sync
        def _(sp):
            for s in range(STREAMS):
                sp.sem_inc(stored[s], 16)

            def load(t, it, s, source):
                sp.wait_ge(xt_psum[s], it + FREED)
                sp.wait_ge(x_keep_ready[s], it + FREED)
                if source is x_mid:
                    sp.wait_ge(stored[s], (it - NT) * 16 + 32)
                sp.dma_start(stage[s][:], source[graphs(t, s), :, :].rearrange("b n d -> n b d")) \
                  .then_inc(loaded[s], 16)
                sp.wait_ge(mask_ready[s], it + FREED)
                sp.dma_start(mask_words[s][:], adj[graphs(t, s), :, :].rearrange("b i j -> i b j")) \
                  .then_inc(mask_loaded[s], 16)

            def store(t, it, s, target):
                sp.wait_ge(x_done[s], it + FULL)
                sp.wait_ge(stored[s], it * 16 + 16)
                sp.dma_start(target[graphs(t, s), :, :].rearrange("b n d -> n b d"),
                             x_new[s][:].rearrange("p (b d) -> p b d", b=GB)).then_inc(stored[s], 16)

            def load_weights(layer, it):
                for s in range(STREAMS):
                    sp.wait_ge(ot_psum[s], it + FREED)
                    sp.wait_ge(x_keep_ready[s], it + FREED)
                sp.dma_start(raw_w, attn_w[bass.ds(layer, 1)].rearrange("l m (c p) o -> p (l m) c o", p=P)) \
                  .then_inc(raw_loaded, 16)
                sp.dma_start(bias_rows[:], attn_bo[bass.ds(layer, 1)].rearrange("l p o -> p (l o)")) \
                  .then_inc(raw_loaded, 16)

            def sweep(layer, source):
                base = layer * NT
                for t in range(2):
                    for s in range(STREAMS):
                        load(t, base + t, s, source)
                with sp.Fori(2, NT) as t:
                    for s in range(STREAMS):
                        load(t, base + t, s, source)
                        store(t - 2, base + t - 2, s, x_mid)
                for t in range(NT - 2, NT):
                    for s in range(STREAMS):
                        store(t, base + t, s, x_mid)

            load_weights(0, 0)
            sweep(0, x)
            with sp.Fori(1, LAYERS) as layer:
                load_weights(layer, layer * NT)
                sweep(layer, x_mid)

            for s in range(STREAMS):
                sp.wait_ge(ot_psum[s], ATTN_ITS + FREED)
                sp.wait_ge(x_done[s], ATTN_ITS + FREED)
            sp.dma_start(raw_w, gcn_w[0:4].rearrange("m (c p) o -> p m c o", p=P)).then_inc(graph_raw_loaded, 16)
            sp.dma_start(raw_g, gcn_w[4].rearrange("(c p) o -> p c o", p=P)).then_inc(graph_raw_loaded, 16)
            sp.dma_start(cols[:], gcn_cols).then_inc(graph_raw_loaded, 16)
            sp.wait_ge(const_ready, 9)
            for r in range(P // DK):
                sp.dma_start(tail_w[r * DK:(r + 1) * DK, r * DK:(r + 1) * DK], gcn_tail).then_inc(graph_raw_loaded, 16)

            def graph_load(t, s):
                sp.wait_ge(xt_psum[s], ATTN_ITS + t + FREED)
                sp.wait_ge(x_keep_ready[s], ATTN_ITS + FREED)
                sp.wait_ge(stored[s], (ATTN_ITS - NT + t) * 16 + 32)
                sp.dma_start(stage[s][:], x_mid[graphs(t, s), :, :].rearrange("b n d -> n b d")).then_inc(loaded[s], 16)
                sp.wait_ge(keep_ready[s], t + FREED)
                sp.wait_ge(mask_ready[s], ATTN_ITS + t + FREED)
                sp.dma_start(mask_words[s][:], adj[graphs(t, s), :, :].rearrange("b i j -> i b j")) \
                  .then_inc(mask_loaded[s], 16)

            def load_keep(t, s):
                sp.wait_ge(y_ready[s], ATTN_ITS + t + FREED)
                sp.dma_start(x_keep[s][:].rearrange("p (b d) -> p b d", b=GB),
                             x_mid[graphs(t, s), :, :].rearrange("b n d -> n b d")).then_inc(kept[s], 16)

            def spread(t, s, part, diag, hi_ready, lo_ready, used, done):
                sp.wait_ge(hi_ready[s], t + FULL)
                sp.wait_ge(lo_ready[s], t + FULL)
                sp.wait_ge(used[s], t * 2 + FREED)
                for r in range(4):
                    rows = slice(r * DK, (r + 1) * DK)
                    sp.dma_start(diag[s][rows, r].rearrange("p w c b j -> p (w c b j)").bitcast(F32),
                                 part[s][rows].rearrange("p w c b j -> p (w c b j)").bitcast(F32)).then_inc(done[s], 16)

            def graph_steps(t, s):
                spread(t, s, k_part, k_diag, k_hi_ready, k_lo_ready, g_scores_psum, k_spread)
                spread(t, s, n_part, n_diag, n_hi_ready, n_lo_ready, g_cos_psum, n_spread)
                load_keep(t, s)

            sp.wait_ge(ones_ready, 7)
            for s in range(STREAMS):
                graph_load(0, s)
            for s in range(STREAMS):
                graph_load(1, s)
                graph_steps(0, s)
            with sp.Fori(2, NT) as t:
                for s in range(STREAMS):
                    graph_load(t, s)
                    graph_steps(t - 1, s)
                    store(t - 2, ATTN_ITS + t - 2, s, out)
            for s in range(STREAMS):
                graph_steps(NT - 1, s)
                store(NT - 2, ATTN_ITS + NT - 2, s, out)
            for s in range(STREAMS):
                store(NT - 1, ATTN_ITS + NT - 1, s, out)
            for s in range(STREAMS):
                sp.wait_ge(stored[s], (ATTN_ITS + NT) * 16 + 16)

        @block.gpsimd
        def _(pool):
            credit(pool, mask_ready, x_keep_ready, keep_ready)
            pool.memset(ident[:], 0.0).then_inc(const_ready, 1)
            pool.wait_ge(const_ready, 1)
            pool.affine_select(out=ident[:], in_=ident[:], compare_op=ALU.not_equal, fill=1.0, base=0,
                               pattern=[[-1, P]], channel_multiplier=1).then_inc(const_ready, 1)
            pool.wait_ge(const_ready, 2)
            pool.tensor_copy(ident_bf[:], ident[:]).then_inc(const_ready, 1)
            pool.memset(tail_w[:], 0.0).then_inc(const_ready, 1)
            pool.memset(head_ones[:], 0.0).then_inc(const_ready, 1)
            pool.wait_ge(const_ready, 5)
            for r in range(P // DK):
                pool.memset(head_ones[r * DK:(r + 1) * DK, r * DK:(r + 1) * DK], 1.0).then_inc(const_ready, 1)
                pool.wait_ge(const_ready, 6 + r)

            with pool.Fori(0, LAYERS) as layer:
                with pool.Fori(0, NT) as t:
                    it = layer * NT + t
                    landed = it * 16 + 16
                    landed_bias = layer * 32 + 32
                    freed = it + FREED
                    for count in (landed, landed_bias, freed):
                        pool.compute_val(count)
                    for s in range(STREAMS):
                        pool.wait_ge(const_ready, 9)
                        pool.wait_ge(mask_loaded[s], landed)
                        pool.wait_ge(scores_psum[s], freed)
                        pool.tensor_scalar(mask_add[s][:], mask_raw[s], -1.0, MASKED, ALU.add, ALU.mult) \
                            .then_inc(mask_ready[s], 1)
                        pool.wait_ge(raw_loaded, landed_bias)
                        pool.wait_ge(loaded[s], landed)
                        pool.wait_ge(y_ready[s], freed)
                        pool.tensor_tensor(x_keep[s][:].rearrange("p (b f) -> p b f", b=GB), stage[s][:],
                                           bias_rows[:].unsqueeze(1).to_broadcast([P, GB, D]), ALU.add) \
                            .then_inc(x_keep_ready[s], 1)

            with pool.Fori(0, NT) as t:
                landed = t * 16 + (ATTN_ITS * 16 + 16)
                summed = t + (ATTN_ITS + FREED)
                added = t * 2 + FREED
                for count in (landed, summed, added):
                    pool.compute_val(count)
                for s in range(STREAMS):
                    pool.wait_ge(const_ready, 9)
                    pool.wait_ge(mask_loaded[s], landed)
                    pool.wait_ge(y_ready[s], summed)
                    pool.tensor_scalar(keep[s][:], mask_raw[s][:, :, 0:1], -1.0, 1.0, ALU.mult, ALU.add) \
                        .then_inc(keep_ready[s], 1)
                    pool.wait_ge(scores_psum[s], ATTN_ITS + FREED)
                    pool.wait_ge(g_scores_psum[s], added)
                    pool.tensor_scalar(mask_add[s][:], mask_raw[s], -MASKED, 0.0, ALU.mult, ALU.add) \
                        .then_inc(mask_ready[s], 1)

        @block.tensor
        def _(pe):
            credit(pe, xt_psum, v_psum, scores_psum, o_psum, ot_psum, wo_psum, g_scores_psum, g_cos_psum, gt_psum)
            credit(pe, q_psum, k_psum, pt_psum, m_psum, ss_psum, g_out_psum)

            def split_product(dst, left, right):
                n = len(SPLIT_PRODUCTS) * DC
                for i, (a, b) in enumerate(SPLIT_PRODUCTS):
                    for c in range(DC):
                        k = i * DC + c
                        last = pe.matmul(dst, left[a](c), right[b](c), start=(k == 0), stop=(k == n - 1))
                return last

            def transpose_rows(s, bank, rows):
                for b in range(GB):
                    for c in range(DC):
                        o = c * GB * N + b * N
                        last = pe.transpose(psum[s][:, bank, o:o + N], rows[:, b, c * P:(c + 1) * P], ident[:])
                return last

            def project_t(s, bank, slot):
                for m in range(DC):
                    last = split_product(
                        psum[s][:, bank, m * GB * N:(m + 1) * GB * N],
                        [lambda c, w=w: w[:, slot, c, m * P:(m + 1) * P] for w in w_part],
                        [lambda c, v=v: v[:, c, :] for v in xt[s]])
                return last

            def project_rows(s, bank, left, slot):
                for b in range(GB):
                    last = split_product(
                        psum[s][:, bank, b * D:(b + 1) * D],
                        [lambda c, v=v: v[:, c, b * N:(b + 1) * N] for v in left],
                        [lambda c, w=w: w[:, slot, c, :] for w in w_part])
                return last

            def transpose_x(it, s):
                pe.wait_ge(loaded[s], it * 16 + 16)
                transpose_rows(s, WK0, stage[s]).then_inc(xt_psum[s], 1)

            def project_qk(it, s, layer):
                pe.wait_ge(w_split, layer + 1)
                pe.wait_ge(xt_hi_ready[s], it + FULL)
                pe.wait_ge(xt_lo_ready[s], it + FULL)
                project_t(s, WK1, WQ).then_inc(q_psum[s], 1)
                pe.wait_ge(ot_hi_ready[s], it + FREED)
                pe.wait_ge(ot_lo_ready[s], it + FREED)
                project_t(s, WK0, WK).then_inc(k_psum[s], 1)

            def project_v(it, s):
                pe.wait_ge(o_ready[s], it + FREED)
                project_rows(s, SC0, xt[s], WV).then_inc(v_psum[s], 1)

            def scores(it, s):
                pe.wait_ge(mask_ready[s], it + FULL)
                pe.wait_ge(q_ready[s], it + FULL)
                pe.wait_ge(k_ready[s], it + FULL)
                for r in (1, 0):
                    if r == 1:
                        pe.wait_ge(y_ready[s], it + FREED)
                    else:
                        pe.wait_ge(v_ready[s], it + FULL)
                    pe.matmul(psum[s][:, SC0 + r, :].rearrange("p (b c j) -> p b c j", b=GB, c=DC), ident_bf[:],
                              mask_add[s][:].unsqueeze(2).to_broadcast([P, GB, DC, N]), start=True, stop=True)
                    for b in range(GB):
                        for c in range(DC):
                            o = (b * DC + c) * N
                            last = pe.matmul(psum[s][:, SC0 + r, o:o + N],
                                             qt[s][r * DH:(r + 1) * DH, c, b * N:(b + 1) * N],
                                             kt[s][r * DH:(r + 1) * DH, c, b * N:(b + 1) * N],
                                             start=False, stop=True, skip_group_check=True)
                last.then_inc(scores_psum[s], 1)

            def transpose_probs(it, s):
                pe.wait_ge(probs_ready[s], it + FULL)
                for b in range(GB):
                    for h in range(H):
                        last = pe.transpose(psum[s][:, WK0 + b, h * N:(h + 1) * N], probs[s][:, b, h, :], ident[:])
                last.then_inc(pt_psum[s], 1)

            def weighted_values(it, s):
                for b in range(GB):
                    pe.wait_ge((pt0_ready, pt1_ready)[b][s], it + FULL)
                    for h in range(H):
                        last = pe.matmul(psum[s][:, SC0 + b, h * (DH + 1):(h + 1) * (DH + 1)],
                                         probs_t[s][:, b, h, :], v_ones[s][:, b, h, :], start=True, stop=True)
                last.then_inc(o_psum[s], 1)

            def transpose_out(it, s, newest):
                pe.wait_ge(o_ready[s], it + FULL)
                pe.wait_ge(xt_hi_ready[s], newest + FULL)
                pe.wait_ge(xt_lo_ready[s], newest + FULL)
                transpose_rows(s, WK0, attn_out[s]).then_inc(ot_psum[s], 1)

            def project_out(it, s):
                pe.wait_ge(ot_hi_ready[s], it + FULL)
                pe.wait_ge(ot_lo_ready[s], it + FULL)
                project_rows(s, SC1, ot[s], WO).then_inc(wo_psum[s], 1)

            def attention(now, nxt, layer):
                newest = now if nxt is None else nxt
                X, Y = range(STREAMS)
                if now is not None:
                    weighted_values(now, X)
                if nxt is not None:
                    transpose_x(nxt, X)
                if now is not None:
                    scores(now, Y)
                    transpose_out(now, X, newest)
                if nxt is not None:
                    project_qk(nxt, X, layer)
                if now is not None:
                    project_out(now, X)
                    transpose_probs(now, Y)
                if nxt is not None:
                    project_v(nxt, X)
                if now is not None:
                    weighted_values(now, Y)
                if nxt is not None:
                    transpose_x(nxt, Y)
                    scores(nxt, X)
                if now is not None:
                    transpose_out(now, Y, newest)
                if nxt is not None:
                    project_qk(nxt, Y, layer)
                if now is not None:
                    project_out(now, Y)
                if nxt is not None:
                    transpose_probs(nxt, X)
                    project_v(nxt, Y)

            def fuse_weights():
                bank = psum[0]
                pe.wait_ge(graph_raw_loaded, 16 * 7)
                pe.wait_ge(gb_wide_ready, 1)
                for i in range(2):
                    for m in range(DC):
                        for c in range(DC):
                            pe.matmul(bank[:, i, m * D:(m + 1) * D], raw_w[:, RAW_M, c, m * P:(m + 1) * P],
                                      raw_w[:, RAW_QT + i, c, :], start=(c == 0), stop=(c == DC - 1))
                for m in range(DC):
                    for c in range(DC):
                        o = m * D + c * P
                        pe.matmul(bank[:, 2, o:o + P], raw_g[:, c, m * P:(m + 1) * P], tail_w[:], start=True, stop=True)
                for i in range(2):
                    for m in range(DC):
                        for c in range(DC):
                            pe.matmul(bank[:, 3, i * DC + m:i * DC + m + 1], raw_w[:, RAW_QT + i, c, m * P:(m + 1) * P],
                                      cols[:, 0, c:c + 1], start=(c == 0), stop=(c == DC - 1))
                for c in range(DC):
                    last = pe.matmul(bank[:, 3, P + c * P:P + (c + 1) * P], gb_wide[:, c, :], tail_w[:],
                                     start=True, stop=True)
                last.then_inc(fused_psum, 1)

            def graph_transpose_x(t, s):
                pe.wait_ge(loaded[s], (ATTN_ITS + t) * 16 + 16)
                transpose_rows(s, 3, stage[s]).then_inc(xt_psum[s], 1)

            def graph_projections(t, s):
                pe.wait_ge(xt_hi_ready[s], ATTN_ITS + t + FULL)
                pe.wait_ge(xt_lo_ready[s], ATTN_ITS + t + FULL)
                project_t(s, 3, WM).then_inc(m_psum[s], 1)
                project_t(s, 0, WMQ).then_inc(q_psum[s], 1)
                project_t(s, 1, WMK).then_inc(k_psum[s], 1)

            def square_sums(t, s):
                pe.wait_ge(y_ready[s], ATTN_ITS + t + FREED)
                pe.wait_ge(sq_ready[s], t + FULL)
                for c in range(DC):
                    last = pe.matmul(psum[s][:, 2, c * GB * N:(c + 1) * GB * N], head_ones[:], kt[s][:, c, :],
                                     start=True, stop=True)
                last.then_inc(ss_psum[s], 1)

            def graph_values(t, s):
                pe.wait_ge(m_ready[s], t + FULL)
                project_rows(s, 3, xt[s], WG).then_inc(v_psum[s], 1)

            def graph_scores(t, s, half):
                if half == 0:
                    pe.wait_ge(mask_ready[s], ATTN_ITS + t + FULL)
                    pe.wait_ge(q_hi_ready[s], t + FULL)
                    pe.wait_ge(q_lo_ready[s], t + FULL)
                    pe.wait_ge(k_spread[s], t * 64 + 64)
                for b in range(GB):
                    pe.matmul(psum[s][:, b, :].rearrange("p (r j) -> p r j", r=4), ident_bf[:],
                              mask_add[s][:, b, :].unsqueeze(1).to_broadcast([P, 4, N]), start=True, stop=True)
                    for left, right in SPLIT_PRODUCTS:
                        last = pe.matmul(psum[s][:, b, :].rearrange("p (r j) -> p r j", r=4), ot[s][left][:, half, b * N:(b + 1) * N],
                                         k_diag[s][:, :, right, half, b],
                                         start=False, stop=True, skip_group_check=True)
                last.then_inc(g_scores_psum[s], 1)

            def graph_cosines(t, s, half):
                if half == 0:
                    pe.wait_ge(n_spread[s], t * 64 + 64)
                    order = ((0, None), (1, v_ready[s]))
                    free_count = ATTN_ITS + t + FULL
                else:
                    order = ((1, None), (0, half_ready[s]))
                    free_count = t + FULL
                for b, bank_free in order:
                    if bank_free is not None:
                        pe.wait_ge(bank_free, free_count)
                    for i, (left, right) in enumerate(SPLIT_PRODUCTS):
                        last = pe.matmul(psum[s][:, 2 + b, :].rearrange("p (r j) -> p r j", r=4), n_part[s][:, left, half, b],
                                         n_diag[s][:, :, right, half, b],
                                         start=(i == 0), stop=(i == len(SPLIT_PRODUCTS) - 1))
                last.then_inc(g_cos_psum[s], 1)

            def transpose_gates(t, s, half):
                for b in range(GB):
                    pe.wait_ge(gate_ready[b][s], t * 2 + half + FULL)
                    for r in range(4):
                        last = pe.transpose(psum[s][:, b, r * N:(r + 1) * N], probs[s][:, b, r, :], ident[:])
                last.then_inc(gt_psum[s], 1)

            def gated_values(t, s, half):
                for b in range(GB):
                    pe.wait_ge(gt_ready[b][s], t * 2 + half + FULL)
                    for r in range(4):
                        o = (b * 4 + r) * (DK + 1)
                        last = pe.matmul(psum[s][:, 2, o:o + DK + 1], probs_t[s][:, b, r, :],
                                         g_ones[s][:, b, 4 * half + r, :], start=True, stop=True)
                last.then_inc(g_out_psum[s], 1)

            def graph(now, nxt):
                for s, other, ending in ((0, 1, now), (1, 0, nxt)):
                    if nxt is not None:
                        graph_transpose_x(nxt, s)
                    if now is not None:
                        gated_values(now, s, 1)
                    if nxt is not None:
                        graph_projections(nxt, s)
                        square_sums(nxt, s)
                    if ending is not None:
                        transpose_gates(ending, other, 0)
                    if nxt is not None:
                        graph_values(nxt, s)
                    if ending is not None:
                        gated_values(ending, other, 0)
                        graph_scores(ending, other, 1)
                        graph_cosines(ending, other, 1)
                    if nxt is not None:
                        graph_scores(nxt, s, 0)
                        graph_cosines(nxt, s, 0)
                    if ending is not None:
                        transpose_gates(ending, other, 1)

            pe.wait_ge(const_ready, 9)
            with pe.Fori(0, LAYERS) as layer:
                first = layer * NT
                attention(None, first, layer)
                with pe.Fori(0, NT - 1) as t:
                    attention(first + t, first + t + 1, layer)
                attention(first + (NT - 1), None, layer)

            for s in range(STREAMS):
                pe.wait_ge(y_ready[s], ATTN_ITS + FREED)
            fuse_weights()
            pe.wait_ge(fused_ready, 1)
            graph(None, 0)
            with pe.Fori(0, NT - 1) as t:
                graph(t, t + 1)
            graph(NT - 1, None)

        @block.scalar
        def _(act):
            credit(act, xt_hi_ready, q_ready, v_ready, probs_ready, pt1_ready, ot_hi_ready, log_ready, rstd_ready,
                   m_ready, sq_ready, ss_log_ready, inv_norm_ready, q_hi_ready, k_hi_ready, n_hi_ready,
                   *g_exp_ready, gt_ready[1])

            def split_hi(it, s, bank):
                act.wait_ge(xt_psum[s], it + FULL)
                act.wait_ge(v_psum[s], it + FREED)
                act.activation(xt[s][HI][:].rearrange("p c n -> p (c n)"), psum[s][:, bank, :], ACT.Copy) \
                   .then_inc(xt_hi_ready[s], 1)

            def xt_hi(it, s):
                split_hi(it, s, WK0)

            def q_out(it, s):
                act.wait_ge(q_psum[s], it + FULL)
                act.activation(qt[s][:].rearrange("p c n -> p (c n)"), psum[s][:, WK1, :], ACT.Copy,
                               scale=float(DH) ** -0.5).then_inc(q_ready[s], 1)

            def v_out(it, s):
                act.wait_ge(v_psum[s], it + FULL)
                act.wait_ge(o_psum[s], it + FREED)
                act.activation(v_ones[s][:, :, :, 0:DH],
                               psum[s][:, SC0, :].rearrange("p (b h d) -> p b h d", b=GB, h=H), ACT.Copy) \
                   .then_inc(v_ready[s], 1)

            def exps(it, s):
                act.wait_ge(max_ready[s], it + FULL)
                act.wait_ge(ot_psum[s], it + FREED)
                for r in range(2):
                    for b in range(GB):
                        for c in range(DC):
                            o = (b * DC + c) * N
                            last = act.activation(probs[s][:, b, 2 * c + r, :], psum[s][:, SC0 + r, o:o + N], ACT.Exp,
                                                  bias=neg_max[s][:, r * 4 + b * DC + c:r * 4 + b * DC + c + 1])
                last.then_inc(probs_ready[s], 1)

            def pt1(it, s):
                act.wait_ge(pt_psum[s], it + FULL)
                act.activation(probs_t[s][:, 1].rearrange("p h i -> p (h i)"), psum[s][:, WK1, :], ACT.Copy) \
                   .then_inc(pt1_ready[s], 1)

            def ot_hi(it, s):
                act.wait_ge(ot_psum[s], it + FULL)
                act.wait_ge(wo_psum[s], it + FREED)
                act.activation(ot[s][HI][:].rearrange("p c n -> p (c n)"), psum[s][:, WK0, :], ACT.Copy) \
                   .then_inc(ot_hi_ready[s], 1)

            def rstd_of(it, s):
                act.wait_ge(mv_ready[s], it + FULL)
                act.activation(log_var[s][:], mean_var[s][:, :, 1], ACT.Ln, bias=eps_col[:, 0:1]) \
                   .then_inc(log_ready[s], 1)
                act.wait_ge(log_ready[s], it + FULL)
                act.activation(rstd[s][:], log_var[s][:], ACT.Exp, scale=-0.5).then_inc(rstd_ready[s], 1)

            def attention(now, nxt):
                X, Y = range(STREAMS)

                def step(what, it, s):
                    if it is not None:
                        what(it, s)

                step(xt_hi, nxt, X)
                step(ot_hi, now, X)
                step(exps, now, Y)
                step(q_out, nxt, X)
                step(pt1, now, Y)
                step(rstd_of, now, X)
                step(v_out, nxt, X)
                step(xt_hi, nxt, Y)
                step(ot_hi, now, Y)
                step(exps, nxt, X)
                step(q_out, nxt, Y)
                step(pt1, nxt, X)
                step(rstd_of, now, Y)
                step(v_out, nxt, Y)

            def m_out(t, s):
                act.wait_ge(m_psum[s], t + FULL)
                act.wait_ge(n_lo_ready[s], t + FREED)
                for c in range(DC):
                    last = act.activation(qt[s][:, c, :], psum[s][:, 3, c * GB * N:(c + 1) * GB * N], ACT.Identity,
                                          bias=cols[:, 0, c:c + 1])
                last.then_inc(m_ready[s], 1)
                act.wait_ge(m_ready[s], t + FULL)
                act.wait_ge(n_ready[s], t + FREED)
                act.activation(flat["sq"][s], flat["m"][s], ACT.Square).then_inc(sq_ready[s], 1)

            def q_hi(t, s):
                act.wait_ge(q_psum[s], ATTN_ITS + t + FULL)
                act.wait_ge(g_scores_psum[s], t * 2 + FREED)
                for c in range(DC):
                    last = act.activation(ot[s][HI][:, c, :], psum[s][:, 0, c * GB * N:(c + 1) * GB * N], ACT.Identity,
                                          bias=fused_b[:, 0, c:c + 1])
                last.then_inc(q_hi_ready[s], 1)

            def k_hi(t, s):
                act.wait_ge(k_psum[s], ATTN_ITS + t + FULL)
                act.wait_ge(g_scores_psum[s], t * 2 + FREED)
                for c in range(DC):
                    last = act.activation(k_part[s][:, HI, c].rearrange("p b n -> p (b n)"),
                                          psum[s][:, 1, c * GB * N:(c + 1) * GB * N], ACT.Identity,
                                          bias=fused_b[:, 1, c:c + 1])
                last.then_inc(k_hi_ready[s], 1)

            def inverse_norms(t, s):
                act.wait_ge(ss_ready[s], t + FULL)
                act.activation(flat["sq"][s], flat["sq"][s], ACT.Ln).then_inc(ss_log_ready[s], 1)
                act.wait_ge(ss_log_ready[s], t + FULL)
                act.activation(flat["sq"][s], flat["sq"][s], ACT.Exp, scale=-0.5).then_inc(inv_norm_ready[s], 1)

            def n_hi(t, s):
                act.wait_ge(n_ready[s], t + FULL)
                act.wait_ge(g_cos_psum[s], t * 2 + FREED)
                act.activation(n_part[s][:, HI].rearrange("p c b n -> p (c b n)"), flat["m"][s], ACT.Copy) \
                   .then_inc(n_hi_ready[s], 1)

            def graph_exps(t, s, half, b):
                act.wait_ge(g_max_ready[b][s], t * 2 + half + FULL)
                if half == 0:
                    act.wait_ge(y_ready[s], ATTN_ITS + t + FREED)
                else:
                    act.wait_ge(gt_psum[s], t * 2 + half + FREED)
                for r in range(4):
                    h = 4 * half + r
                    last = act.activation(probs[s][:, b, r, :], psum[s][:, b, r * N:(r + 1) * N], ACT.Exp,
                                          bias=neg_max[s][:, b * 4 + r:b * 4 + r + 1],
                                          accum_out=row_sum[s][:, b, h:h + 1])
                last.then_inc(g_exp_ready[b][s], 1)

            def gt1(t, s, half):
                act.wait_ge(gt_psum[s], t * 2 + half + FULL)
                act.activation(probs_t[s][:, 1].rearrange("p r i -> p (r i)"), psum[s][:, 1, :], ACT.Copy) \
                   .then_inc(gt_ready[1][s], 1)

            def graph(now, nxt):
                for s, other, ending in ((0, 1, now), (1, 0, nxt)):
                    if ending is not None:
                        graph_exps(ending, other, 0, 0)
                    if now is not None:
                        gt1(now, s, 1)
                    if nxt is not None:
                        split_hi(ATTN_ITS + nxt, s, 3)
                    if ending is not None:
                        graph_exps(ending, other, 0, 1)
                    if nxt is not None:
                        m_out(nxt, s)
                        q_hi(nxt, s)
                        k_hi(nxt, s)
                        inverse_norms(nxt, s)
                    if ending is not None:
                        gt1(ending, other, 0)
                    if nxt is not None:
                        n_hi(nxt, s)
                    if now is not None:
                        rstd_of(ATTN_ITS + now, s)
                    if ending is not None:
                        graph_exps(ending, other, 1, 0)
                        graph_exps(ending, other, 1, 1)

            act.preload_act_table_set("natural_log_exp_and_others")
            act.wait_ge(ones_ready, 7)
            with act.Fori(0, LAYERS) as layer:
                first = layer * NT
                attention(None, first)
                with act.Fori(0, NT - 1) as t:
                    attention(first + t, first + t + 1)
                attention(first + (NT - 1), None)
            act.wait_ge(graph_raw_loaded, 16 * 7)
            graph(None, 0)
            with act.Fori(0, NT - 1) as t:
                graph(t, t + 1)
            graph(NT - 1, None)

        @block.vector
        def _(dve):
            credit(dve, xt_lo_ready, k_ready, max_ready, pt0_ready, rcp_ready, o_ready, ot_lo_ready, y_ready, bn_ready,
                   mv_ready, x_done, ss_ready, n_ready, q_lo_ready, k_lo_ready, n_lo_ready, *g_max_ready,
                   *gate_ready, gt_ready[0], half_ready, total_ready, g_rcp_ready, g_scale_ready, scaled_ready)

            def split_lo(it, s, bank):
                dve.wait_ge(xt_hi_ready[s], it + FULL)
                dve.tensor_tensor(xt[s][LO][:].rearrange("p c n -> p (c n)"), psum[s][:, bank, :],
                                  xt[s][HI][:].rearrange("p c n -> p (c n)").bitcast(F32), ALU.subtract) \
                   .then_inc(xt_lo_ready[s], 1)

            def xt_lo(it, s):
                split_lo(it, s, WK0)

            def k_out(it, s):
                dve.wait_ge(k_psum[s], it + FULL)
                dve.tensor_copy(kt[s][:].rearrange("p c n -> p (c n)"), psum[s][:, WK0, :]).then_inc(k_ready[s], 1)

            def maxima(it, s):
                dve.wait_ge(scores_psum[s], it + FULL)
                dve.wait_ge(probs_ready[s], it + FREED)
                dve.tensor_reduce(neg_max[s][:].rearrange("p (r q) -> p r q", r=2),
                                  psum[s][:, SC0:SC1 + 1, :].rearrange("p r (q j) -> p r q j", j=N),
                                  AX_X, ALU.max, negate=True).then_inc(max_ready[s], 1)

            def pt0(it, s):
                dve.wait_ge(pt_psum[s], it + FULL)
                dve.tensor_copy(probs_t[s][:, 0].rearrange("p h i -> p (h i)"), psum[s][:, WK0, :]) \
                   .then_inc(pt0_ready[s], 1)

            def normalise(it, s):
                sums = psum[s][:, SC0:SC1 + 1, 0:H * (DH + 1)].rearrange("p b (h d) -> p b h d", h=H)
                r = rcp[s][:, 0:GB * H].rearrange("p (b h) -> p b h", b=GB)
                dve.wait_ge(o_psum[s], it + FULL)
                dve.reciprocal(r, sums[:, :, :, DH]).then_inc(rcp_ready[s], 1)
                dve.wait_ge(rcp_ready[s], it + FULL)
                dve.tensor_tensor(attn_out[s].rearrange("p b (h d) -> p b h d", h=H), sums[:, :, :, 0:DH],
                                  r.unsqueeze(3).to_broadcast([P, GB, H, DH]), ALU.mult).then_inc(o_ready[s], 1)

            def ot_lo(it, s):
                dve.wait_ge(ot_hi_ready[s], it + FULL)
                dve.tensor_tensor(ot[s][LO][:].rearrange("p c n -> p (c n)"), psum[s][:, WK0, :],
                                  ot[s][HI][:].rearrange("p c n -> p (c n)").bitcast(F32), ALU.subtract) \
                   .then_inc(ot_lo_ready[s], 1)

            def residual(it, s):
                dve.wait_ge(wo_psum[s], it + FULL)
                dve.wait_ge(x_keep_ready[s], it + FULL)
                dve.tensor_tensor(y_sum[s], psum[s][:, SC1, :], x_keep[s][:], ALU.add).then_inc(y_ready[s], 1)

            def statistics(it, s):
                dve.wait_ge(y_ready[s], it + FULL)
                for b in range(GB):
                    last = dve.bn_stats(bn[s][:, b, :], y_sum[s][:, b * D:(b + 1) * D])
                last.then_inc(bn_ready[s], 1)
                dve.wait_ge(ones_ready, 7)
                dve.wait_ge(bn_ready[s], it + FULL)
                for b in range(GB):
                    last = dve.bn_aggr(mean_var[s][:, b, :], bn[s][:, b, :])
                last.then_inc(mv_ready[s], 1)

            def norm_rows(it, s):
                dve.wait_ge(rstd_ready[s], it + FULL)
                dve.wait_ge(stored[s], it * 16 + 16)
                for b in range(GB):
                    last = dve.tensor_scalar(x_new[s][:, b * D:(b + 1) * D], y_sum[s][:, b * D:(b + 1) * D],
                                             mean_var[s][:, b, 0:1], rstd[s][:, b:b + 1], ALU.subtract, ALU.mult)
                last.then_inc(x_done[s], 1)

            def attention(now, nxt):
                X, Y = range(STREAMS)

                def step(what, it, s):
                    if it is not None:
                        what(it, s)

                step(normalise, now, X)
                step(xt_lo, nxt, X)
                step(maxima, now, Y)
                step(ot_lo, now, X)
                step(k_out, nxt, X)
                step(residual, now, X)
                step(pt0, now, Y)
                step(statistics, now, X)
                step(norm_rows, now, X)
                step(normalise, now, Y)
                step(xt_lo, nxt, Y)
                step(maxima, nxt, X)
                step(ot_lo, now, Y)
                step(k_out, nxt, Y)
                step(residual, now, Y)
                step(pt0, nxt, X)
                step(statistics, now, Y)
                step(norm_rows, now, Y)

            def split_fused():
                bank = psum[0]
                dve.wait_ge(fused_psum, 1)
                flat_w = [w[:].rearrange("p m c o -> p m (c o)") for w in w_part]
                dve.tensor_copy(flat_w[HI][:, WM, :], raw_w[:, RAW_MT].rearrange("p c o -> p (c o)"))
                dve.tensor_scalar(flat_w[HI][:, WMQ, :], bank[:, 0, :], GSCALE, None, ALU.mult)
                dve.tensor_copy(flat_w[HI][:, WMK:WG + 1, :], bank[:, 1:3, :]).then_inc(fused_hi_ready, 1)
                for c in range(DC):
                    dve.tensor_scalar(fused_b[:, 0, c:c + 1], bank[:, 3, c:c + 1], cols[:, 1, c:c + 1], GSCALE,
                                      ALU.add, ALU.mult)
                dve.tensor_tensor(fused_b[:, 1, :], bank[:, 3, DC:2 * DC], cols[:, 2, :], ALU.add)
                dve.tensor_copy(bias_rows[:], bank[:, 3, P:P + D])
                dve.wait_ge(fused_hi_ready, 1)
                dve.tensor_tensor(flat_w[LO][:, WM, :], raw_w[:, RAW_MT].rearrange("p c o -> p (c o)"),
                                  flat_w[HI][:, WM, :].bitcast(F32), ALU.subtract)
                dve.scalar_tensor_tensor(flat_w[LO][:, WMQ, :], bank[:, 0, :], GSCALE,
                                         flat_w[HI][:, WMQ, :].bitcast(F32), ALU.mult, ALU.subtract)
                dve.tensor_tensor(flat_w[LO][:, WMK:WG + 1, :], bank[:, 1:3, :],
                                  flat_w[HI][:, WMK:WG + 1, :].bitcast(F32), ALU.subtract)
                for s in range(STREAMS):
                    last = dve.memset(g_ones[s][:, :, :, DK:DK + 1], 1.0)
                last.then_inc(fused_ready, 1)
                dve.wait_ge(fused_ready, 1)

            def q_lo(t, s):
                dve.wait_ge(q_hi_ready[s], t + FULL)
                for c in range(DC):
                    last = dve.scalar_tensor_tensor(ot[s][LO][:, c, :], psum[s][:, 0, c * GB * N:(c + 1) * GB * N],
                                                    fused_b[:, 0, c:c + 1], ot[s][HI][:, c, :].bitcast(F32),
                                                    ALU.add, ALU.subtract)
                last.then_inc(q_lo_ready[s], 1)

            def k_lo(t, s):
                dve.wait_ge(k_hi_ready[s], t + FULL)
                for c in range(DC):
                    last = dve.scalar_tensor_tensor(k_part[s][:, LO, c].rearrange("p b n -> p (b n)"),
                                                    psum[s][:, 1, c * GB * N:(c + 1) * GB * N], fused_b[:, 1, c:c + 1],
                                                    k_part[s][:, HI, c].rearrange("p b n -> p (b n)").bitcast(F32),
                                                    ALU.add, ALU.subtract)
                last.then_inc(k_lo_ready[s], 1)

            def norm_guard(t, s):
                dve.wait_ge(ss_psum[s], t + FULL)
                dve.tensor_scalar(flat["sq"][s], psum[s][:, 2, :], NORM2_MIN, None, ALU.max).then_inc(ss_ready[s], 1)

            def normalised(t, s):
                dve.wait_ge(inv_norm_ready[s], t + FULL)
                dve.tensor_tensor(flat["m"][s], flat["m"][s], flat["sq"][s], ALU.mult).then_inc(n_ready[s], 1)

            def n_lo(t, s):
                dve.wait_ge(n_hi_ready[s], t + FULL)
                dve.tensor_tensor(n_part[s][:, LO].rearrange("p c b n -> p (c b n)"), flat["m"][s],
                                  n_part[s][:, HI].rearrange("p c b n -> p (c b n)").bitcast(F32), ALU.subtract) \
                   .then_inc(n_lo_ready[s], 1)

            def graph_v(t, s):
                dve.wait_ge(v_psum[s], ATTN_ITS + t + FULL)
                dve.wait_ge(g_out_psum[s], t * 2 + FREED)
                dve.tensor_tensor(g_ones[s][:, :, :, 0:DK],
                                  psum[s][:, 3, :].rearrange("p (b h d) -> p b h d", b=GB, h=GH),
                                  bias_rows[:].rearrange("p (h d) -> p h d", h=GH).unsqueeze(1)
                                  .to_broadcast([P, GB, GH, DK]), ALU.add).then_inc(v_ready[s], 1)

            def graph_maxima(t, s, half, b):
                dve.wait_ge(g_scores_psum[s], t * 2 + half + FULL)
                dve.wait_ge(g_exp_ready[b][s], t * 2 + half + FREED)
                dve.tensor_reduce(neg_max[s][:, b * 4:(b + 1) * 4], psum[s][:, b, :].rearrange("p (r j) -> p r j", r=4),
                                  AX_X, ALU.max, negate=True).then_inc(g_max_ready[b][s], 1)

            def gate(t, s, half, b):
                e = probs[s][:, b].rearrange("p r j -> p (r j)")
                dve.wait_ge(g_exp_ready[b][s], t * 2 + half + FULL)
                dve.wait_ge(g_cos_psum[s], t * 2 + half + FULL)
                dve.scalar_tensor_tensor(e, psum[s][:, 2 + b, :], THRESHOLD, e, ALU.is_gt, ALU.mult) \
                   .then_inc(gate_ready[b][s], 1)

            def gt0(t, s, half):
                dve.wait_ge(gt_psum[s], t * 2 + half + FULL)
                dve.tensor_copy(probs_t[s][:, 0].rearrange("p r i -> p (r i)"), psum[s][:, 0, :]) \
                   .then_inc(gt_ready[0][s], 1)

            HALF = GB * 4 * (DK + 1)

            def first_half(t, s):
                dve.wait_ge(g_out_psum[s], t * 2 + FULL)
                dve.tensor_copy(half_out[s][:], psum[s][:, 2, 0:HALF]).then_inc(half_ready[s], 1)

            def graph_output(t, s):
                halves = [h.rearrange("p (b r d) -> p b r d", b=GB, r=4)
                          for h in (half_out[s][:], psum[s][:, 2, 0:HALF])]
                tot = total[s][:].rearrange("p (b h) -> p b h", b=GB)
                inv = rcp[s][:].rearrange("p (b h) -> p b h", b=GB)
                scaled = probs_all[:, s, 0:GF].rearrange("p (b h d) -> p b h d", b=GB, h=GH)
                dve.wait_ge(g_out_psum[s], t * 2 + 1 + FULL)
                dve.wait_ge(half_ready[s], t + FULL)
                for i in range(2):
                    last = dve.tensor_tensor(tot[:, :, 4 * i:4 * i + 4], halves[i][:, :, :, DK],
                                             row_sum[s][:, :, 4 * i:4 * i + 4], ALU.add)
                last.then_inc(total_ready[s], 1)
                dve.wait_ge(total_ready[s], t + FULL)
                dve.reciprocal(rcp[s][:], total[s][:]).then_inc(g_rcp_ready[s], 1)
                dve.wait_ge(g_rcp_ready[s], t + FULL)
                dve.wait_ge(keep_ready[s], t + FULL)
                dve.tensor_tensor(tot, inv, keep[s][:].to_broadcast([P, GB, GH]), ALU.mult).then_inc(g_scale_ready[s], 1)
                dve.wait_ge(g_scale_ready[s], t + FULL)
                for i in range(2):
                    last = dve.tensor_tensor(scaled[:, :, 4 * i:4 * i + 4, :], halves[i][:, :, :, 0:DK],
                                             tot[:, :, 4 * i:4 * i + 4].unsqueeze(3).to_broadcast([P, GB, 4, DK]),
                                             ALU.mult)
                last.then_inc(scaled_ready[s], 1)
                dve.wait_ge(scaled_ready[s], t + FULL)
                dve.wait_ge(kept[s], t * 16 + 16)
                dve.scalar_tensor_tensor(y_sum[s], probs_all[:, s, 0:GF], 0.0, x_keep[s][:], ALU.max, ALU.add) \
                   .then_inc(y_ready[s], 1)

            def graph(now, nxt):
                for s, other, ending in ((0, 1, now), (1, 0, nxt)):
                    if ending is not None:
                        graph_maxima(ending, other, 0, 1)
                    if now is not None:
                        gt0(now, s, 1)
                    if nxt is not None:
                        split_lo(ATTN_ITS + nxt, s, 3)
                    if ending is not None:
                        gate(ending, other, 0, 0)
                    if now is not None:
                        graph_output(now, s)
                    if ending is not None:
                        gate(ending, other, 0, 1)
                    if nxt is not None:
                        norm_guard(nxt, s)
                        k_lo(nxt, s)
                    if ending is not None:
                        gt0(ending, other, 0)
                    if nxt is not None:
                        normalised(nxt, s)
                        q_lo(nxt, s)
                        n_lo(nxt, s)
                    if ending is not None:
                        first_half(ending, other)
                    if now is not None:
                        statistics(ATTN_ITS + now, s)
                    if ending is not None:
                        graph_maxima(ending, other, 1, 0)
                        graph_maxima(ending, other, 1, 1)
                    if nxt is not None:
                        graph_v(nxt, s)
                    if ending is not None:
                        gate(ending, other, 1, 0)
                    if now is not None:
                        norm_rows(ATTN_ITS + now, s)
                    if nxt is not None:
                        graph_maxima(nxt, s, 0, 0)
                    if ending is not None:
                        gate(ending, other, 1, 1)

            dve.memset(eps_col[:], LN_EPS).then_inc(ones_ready, 1)
            for s in range(STREAMS):
                dve.memset(v_buf[s][:], 1.0).then_inc(ones_ready, 1)
            for s in range(STREAMS):
                for diag in (k_diag, n_diag):
                    dve.memset(diag[s][:].rearrange("p r w c b j -> p (r w c b j)").bitcast(F32), 0.0) \
                       .then_inc(ones_ready, 1)
            with dve.Fori(0, LAYERS) as layer:
                first = layer * NT
                dve.wait_ge(raw_loaded, layer * 32 + 32)
                for s in range(STREAMS):
                    dve.wait_ge(wo_psum[s], first + FREED)
                hi = w_part[HI][:].rearrange("p m c o -> p (m c o)")
                lo = w_part[LO][:].rearrange("p m c o -> p (m c o)")
                raw = raw_w.rearrange("p m c o -> p (m c o)")
                dve.tensor_copy(hi, raw).then_inc(w_hi_ready, 1)
                dve.wait_ge(w_hi_ready, layer + 1)
                dve.tensor_tensor(lo, raw, hi.bitcast(F32), ALU.subtract).then_inc(w_split, 1)
                attention(None, first)
                with dve.Fori(0, NT - 1) as t:
                    attention(first + t, first + t + 1)
                attention(first + (NT - 1), None)

            dve.wait_ge(graph_raw_loaded, 16 * 7)
            for c in range(DC):
                last = dve.tensor_copy(gb_wide[:, c, :], cols[:, 3, c:c + 1].to_broadcast([P, P]))
            last.then_inc(gb_wide_ready, 1)
            for s in range(STREAMS):
                dve.wait_ge(x_keep_ready[s], ATTN_ITS + FREED)
            split_fused()
            graph(None, 0)
            with dve.Fori(0, NT - 1) as t:
                graph(t, t + 1)
            graph(NT - 1, None)


def kernel(x, adj, **w):
    import numpy as np
    import concourse.bacc as bacc
    from concourse.bass_utils import run_bass_kernel_spmd

    def arr(name):
        return np.asarray(w[name])

    x = np.ascontiguousarray(np.asarray(x))
    D = x.shape[2]
    P = 128
    attn = range(3)
    arrays = {
        "x": x,
        "adj": np.ascontiguousarray(np.asarray(adj)).view(np.int32),
        "attn_w": np.stack([np.stack([arr(f"L{l}_gnn_{m}") for m in ("Wq", "Wk", "Wv", "Wo")]) for l in attn]),
        "attn_bo": np.ascontiguousarray(np.broadcast_to(np.stack([arr(f"L{l}_gnn_bo") for l in attn])[:, None], (3, P, D))),
        "gcn_w": np.stack([arr("L3_gnn_map_w").T, arr("L3_gnn_map_w"), arr("L3_gnn_q_w").T, arr("L3_gnn_k_w").T,
                           arr("L3_gnn_gcn_map_w")]),
        "gcn_cols": np.ascontiguousarray(np.stack([arr(f"L3_gnn_{b}") for b in ("map_b", "q_b", "k_b", "gcn_map_b")])
                                         .reshape(4, D // P, P).transpose(2, 0, 1)),
        "gcn_tail": np.ascontiguousarray(arr("L3_gnn_gcn_W").T),
    }
    nc = bacc.Bacc("TRN2", target_bir_lowering=False, num_devices=1)
    args = [nc.dram_tensor(f"in_{n}", a.shape, mybir.dt.from_np(a.dtype), kind="ExternalInput").ap()
            for n, a in arrays.items()]
    out = nc.dram_tensor("out", x.shape, F32, kind="ExternalOutput").ap()
    build(nc, *args, out)
    r = run_bass_kernel_spmd(nc, [{f"in_{n}": a for n, a in arrays.items()}], core_ids=[0])
    return r.results[0]["out"]
```

```python
from contextlib import ExitStack

import concourse.bass as bass
from concourse import mybir

F32 = mybir.dt.float32
F32R = mybir.dt.float32r
BF16 = mybir.dt.bfloat16
U8 = mybir.dt.uint8
I32 = mybir.dt.int32
ALU = mybir.AluOpType
ACT = mybir.ActivationFunctionType
AX_X = mybir.AxisListType.X

P = 128
STREAMS = 2
GB = 2
MASKED = 2.0 ** 100
LN_EPS = 1e-5

HI, LO = 0, 1
SPLIT_PRODUCTS = [(HI, HI), (HI, LO), (LO, HI)]


def build(nc, x, adj, attn_w, attn_bo, gcn_w, gcn_cols, gcn_tail, out):
    B, N, D = x.shape
    LAYERS = attn_w.shape[0]
    H, DH = 4, 64
    GH, DK = 8, 32
    DC = D // P
    NT = B // (GB * STREAMS)
    GF = GB * D
    THRESHOLD = 0.1
    GSCALE = float(DK) ** -0.5
    NORM2_MIN = 1e-16
    assert N == P and DC == 2 and H * DH == D and GH * DK == D
    WQ, WK, WV, WO = range(4)
    WM, WMQ, WMK, WG = range(4)
    RAW_MT, RAW_M, RAW_QT, RAW_KT = range(4)

    with ExitStack() as ctx:
        def sb(name, shape, dt=F32):
            return ctx.enter_context(nc.sbuf_tensor(name, shape, dt))

        def sem(name):
            return ctx.enter_context(nc.semaphore(name))

        def sems(name):
            return [sem(f"{name}{s}") for s in range(STREAMS)]

        w_part = [sb("w_hi", [P, 4, DC, D], F32R), sb("w_lo", [P, 4, DC, D], F32R)]
        bias_rows = sb("bias_rows", [P, D])
        ident = sb("ident", [P, P])
        ident_bf = sb("ident_bf", [P, P], BF16)
        head_ones = sb("head_ones", [P, P])
        tail_w = sb("tail_w", [P, P])
        cols = sb("cols", [P, 4, DC])
        fused_b = sb("fused_b", [P, 2, DC])
        gb_wide = sb("gb_wide", [P, DC, P])
        eps_col = sb("eps_col", [P, 1])

        def per_stream(name, shape, dt=F32):
            return [sb(f"{name}{s}", shape, dt) for s in range(STREAMS)]

        stage = per_stream("stage", [P, GB, D])
        y_sum = per_stream("y_sum", [P, GF])
        x_keep = per_stream("x_keep", [P, GF])
        x_new = per_stream("x_new", [P, GF])
        xt = [[sb(f"xt_hi{s}", [P, DC, GB * N], F32R), sb(f"xt_lo{s}", [P, DC, GB * N], F32R)]
              for s in range(STREAMS)]
        ot = [[sb(f"ot_hi{s}", [P, DC, GB * N], F32R), sb(f"ot_lo{s}", [P, DC, GB * N], F32R)]
              for s in range(STREAMS)]
        qt = per_stream("qt", [P, DC, GB * N])
        kt = per_stream("kt", [P, DC, GB * N])
        v_buf = per_stream("v_buf", [P, GB * GH * (DK + 1)])
        probs_all = sb("probs_all", [P, STREAMS, GB * H * N])
        probs_t_all = sb("probs_t_all", [P, STREAMS, GB * H * N])
        k_part = per_stream("k_part", [P, 2, DC, GB, N], F32R)
        n_part = per_stream("n_part", [P, 2, DC, GB, N], F32R)
        pair_diag = per_stream("pair_diag", [P, 2, 2, DC, GB, N], F32R)
        k_diag = per_stream("k_diag", [P, 4, 2, DC, GB, N], F32R)
        n_diag = per_stream("n_diag", [P, 4, 2, DC, GB, N], F32R)
        mask_words = per_stream("mask_words", [P, GB, N // 4], I32)
        mask_raw = [mask_words[s][:].bitcast(U8) for s in range(STREAMS)]
        mask_add = per_stream("mask_add", [P, GB, N], BF16)
        neg_max = per_stream("neg_max", [P, 8])
        row_sum = per_stream("row_sum", [P, GB, GH])
        half_out = per_stream("half_out", [P, GB * 4 * (DK + 1)])
        rcp = per_stream("rcp", [P, GB * GH])
        total = per_stream("total", [P, GB * GH])
        keep = per_stream("keep", [P, GB, 1])
        bn = per_stream("bn", [P, GB, 6])
        mean_var = per_stream("mean_var", [P, GB, 2])
        log_var = per_stream("log_var", [P, GB])
        rstd = per_stream("rstd", [P, GB])

        raw_w = probs_all[:].rearrange("p s (m c o) -> p (s m) c o", m=2, c=DC)
        raw_g = probs_t_all[:, 0, 0:DC * D].rearrange("p (c o) -> p c o", c=DC)
        probs = [probs_all[:, s].rearrange("p (b h j) -> p b h j", b=GB, h=H) for s in range(STREAMS)]
        probs_t = [probs_t_all[:, s].rearrange("p (b h i) -> p b h i", b=GB, h=H) for s in range(STREAMS)]
        v_rows = [v_buf[s][:, 0:GF] for s in range(STREAMS)]
        g_ones = [v_buf[s][:].rearrange("p (b h d) -> p b h d", b=GB, h=GH) for s in range(STREAMS)]
        flat = {name: [v[s][:].rearrange("p c n -> p (c n)") for s in range(STREAMS)]
                for name, v in (("m", qt), ("sq", kt))}

        psum = [ctx.enter_context(nc.psum_tensor(f"psum{s}", [P, 4, 512], F32)) for s in range(STREAMS)]
        SC0, SC1, WK0, WK1 = range(4)

        x_mid = nc.dram_tensor("x_mid", [B, N, D], F32, kind="Internal").ap()

        FREED, FULL = 1, 2
        loaded = sems("loaded")
        mask_loaded = sems("mask_loaded")
        kept = sems("kept")
        stored = sems("stored")
        const_ready = sem("const_ready")
        ones_ready = sem("ones_ready")
        raw_loaded = sem("raw_loaded")
        w_hi_ready = sem("w_hi_ready")
        w_split = sem("w_split")
        mask_ready = sems("mask_ready")
        x_keep_ready = sems("x_keep_ready")
        xt_psum = sems("xt_psum")
        xt_hi_ready, xt_lo_ready = sems("xt_hi_ready"), sems("xt_lo_ready")
        q_psum, k_psum, v_psum = sems("q_psum"), sems("k_psum"), sems("v_psum")
        v_ready = sems("v_ready")
        q_hi_ready, q_lo_ready = sems("q_hi_ready"), sems("q_lo_ready")
        k_hi_ready, k_lo_ready = sems("k_hi_ready"), sems("k_lo_ready")
        scores_psum = [sems(f"scores{b}_psum") for b in range(GB)]
        max_ready = [sems(f"max{b}_ready") for b in range(GB)]
        exp_ready = [sems(f"exp{b}_ready") for b in range(GB)]
        rcp_ready = [sems(f"rcp{b}_ready") for b in range(GB)]
        probs_ready = [sems(f"probs{b}_ready") for b in range(GB)]
        pt_psum = [sems(f"pt{b}_psum") for b in range(GB)]
        pt_ready = [sems(f"pt{b}_ready") for b in range(GB)]
        o_psum = sems("o_psum")
        ot_hi_ready, ot_lo_ready = sems("ot_hi_ready"), sems("ot_lo_ready")
        wo_psum = sems("wo_psum")
        y_ready = sems("y_ready")
        bn_ready, mv_ready = sems("bn_ready"), sems("mv_ready")
        log_ready, rstd_ready = sems("log_ready"), sems("rstd_ready")
        x_done = sems("x_done")
        graph_raw_loaded = sem("graph_raw_loaded")
        gb_wide_ready = sem("gb_wide_ready")
        fused_psum, fused_hi_ready, fused_ready = sem("fused_psum"), sem("fused_hi_ready"), sem("fused_ready")
        keep_ready = sems("keep_ready")
        m_psum, m_ready, sq_ready = sems("m_psum"), sems("m_ready"), sems("sq_ready")
        ss_psum, ss_ready, ss_log_ready = sems("ss_psum"), sems("ss_ready"), sems("ss_log_ready")
        inv_norm_ready, n_ready = sems("inv_norm_ready"), sems("n_ready")
        n_hi_ready, n_lo_ready = sems("n_hi_ready"), sems("n_lo_ready")
        k_spread, n_spread = sems("k_spread"), sems("n_spread")
        g_scores_psum, g_cos_psum = sems("g_scores_psum"), sems("g_cos_psum")
        g_max_ready = [sems(f"g_max{b}_ready") for b in range(GB)]
        g_exp_ready = [sems(f"g_exp{b}_ready") for b in range(GB)]
        gate_ready = [sems(f"gate{b}_ready") for b in range(GB)]
        gt_psum = [sems(f"gt{b}_psum") for b in range(GB)]
        gt_ready = [sems(f"gt{b}_ready") for b in range(GB)]
        g_out_psum = sems("g_out_psum")
        half_ready = sems("half_ready")
        total_ready = sems("total_ready")
        g_rcp_ready, g_scale_ready = sems("g_rcp_ready"), sems("g_scale_ready")
        scaled_ready = sems("scaled_ready")

        ATTN_ITS = LAYERS * NT

        block = ctx.enter_context(nc.Block())

        def graphs(t, s):
            return bass.ds(t * (STREAMS * GB) + s * GB, GB)

        def credit(eng, *families):
            for family in families:
                for one in family:
                    eng.sem_inc(one, 1)

        @block.sync
        def _(sp):
            for s in range(STREAMS):
                sp.sem_inc(stored[s], 16)

            def load(t, it, s, source):
                sp.wait_ge(xt_psum[s], it + FREED)
                sp.wait_ge(x_keep_ready[s], it + FREED)
                if source is x_mid:
                    sp.wait_ge(stored[s], (it - NT) * 16 + 32)
                sp.dma_start(stage[s][:], source[graphs(t, s), :, :].rearrange("b n d -> n b d")) \
                  .then_inc(loaded[s], 16)
                sp.wait_ge(mask_ready[s], it + FREED)
                sp.dma_start(mask_words[s][:], adj[graphs(t, s), :, :].rearrange("b i j -> i b j")) \
                  .then_inc(mask_loaded[s], 16)

            def store(t, it, s, target):
                sp.wait_ge(x_done[s], it + FULL)
                sp.wait_ge(stored[s], it * 16 + 16)
                sp.dma_start(target[graphs(t, s), :, :].rearrange("b n d -> n b d"),
                             x_new[s][:].rearrange("p (b d) -> p b d", b=GB)).then_inc(stored[s], 16)

            def load_weights(layer, it):
                for s in range(STREAMS):
                    sp.wait_ge(pt_psum[GB - 1][s], it + FREED)
                    sp.wait_ge(x_keep_ready[s], it + FREED)
                sp.dma_start(raw_w, attn_w[bass.ds(layer, 1)].rearrange("l m (c p) o -> p (l m) c o", p=P)) \
                  .then_inc(raw_loaded, 16)
                sp.dma_start(bias_rows[:], attn_bo[bass.ds(layer, 1)].rearrange("l p o -> p (l o)")) \
                  .then_inc(raw_loaded, 16)

            def sweep(layer, source):
                base = layer * NT
                for t in range(2):
                    for s in range(STREAMS):
                        load(t, base + t, s, source)
                with sp.Fori(2, NT) as t:
                    for s in range(STREAMS):
                        load(t, base + t, s, source)
                        store(t - 2, base + t - 2, s, x_mid)
                for t in range(NT - 2, NT):
                    for s in range(STREAMS):
                        store(t, base + t, s, x_mid)

            load_weights(0, 0)
            sweep(0, x)
            with sp.Fori(1, LAYERS) as layer:
                load_weights(layer, layer * NT)
                sweep(layer, x_mid)

            for s in range(STREAMS):
                sp.wait_ge(pt_psum[GB - 1][s], ATTN_ITS + FREED)
                sp.wait_ge(x_done[s], ATTN_ITS + FREED)
            sp.dma_start(raw_w, gcn_w[0:4].rearrange("m (c p) o -> p m c o", p=P)).then_inc(graph_raw_loaded, 16)
            sp.dma_start(raw_g, gcn_w[4].rearrange("(c p) o -> p c o", p=P)).then_inc(graph_raw_loaded, 16)
            sp.dma_start(cols[:], gcn_cols).then_inc(graph_raw_loaded, 16)
            sp.wait_ge(const_ready, 9)
            for r in range(P // DK):
                sp.dma_start(tail_w[r * DK:(r + 1) * DK, r * DK:(r + 1) * DK], gcn_tail).then_inc(graph_raw_loaded, 16)

            def graph_load(t, s):
                sp.wait_ge(xt_psum[s], ATTN_ITS + t + FREED)
                sp.wait_ge(x_keep_ready[s], ATTN_ITS + FREED)
                sp.wait_ge(stored[s], (ATTN_ITS - NT + t) * 16 + 32)
                sp.dma_start(stage[s][:], x_mid[graphs(t, s), :, :].rearrange("b n d -> n b d")).then_inc(loaded[s], 16)
                sp.wait_ge(keep_ready[s], t + FREED)
                sp.wait_ge(mask_ready[s], ATTN_ITS + t + FREED)
                sp.dma_start(mask_words[s][:], adj[graphs(t, s), :, :].rearrange("b i j -> i b j")) \
                  .then_inc(mask_loaded[s], 16)

            def load_keep(t, s):
                sp.wait_ge(y_ready[s], ATTN_ITS + t + FREED)
                sp.dma_start(x_keep[s][:].rearrange("p (b d) -> p b d", b=GB),
                             x_mid[graphs(t, s), :, :].rearrange("b n d -> n b d")).then_inc(kept[s], 16)

            def spread(t, s, count, part, diag, hi_ready, lo_ready, used, done):
                sp.wait_ge(hi_ready[s], count + FULL)
                sp.wait_ge(lo_ready[s], count + FULL)
                sp.wait_ge(used[s], t * 2 + FREED)
                for r in range(4):
                    rows = slice(r * DK, (r + 1) * DK)
                    sp.dma_start(diag[s][rows, r].rearrange("p w c b j -> p (w c b j)").bitcast(F32),
                                 part[s][rows].rearrange("p w c b j -> p (w c b j)").bitcast(F32)).then_inc(done[s], 16)

            def graph_steps(t, s):
                spread(t, s, ATTN_ITS + t, k_part, k_diag, k_hi_ready, k_lo_ready, g_scores_psum, k_spread)
                spread(t, s, t, n_part, n_diag, n_hi_ready, n_lo_ready, g_cos_psum, n_spread)
                load_keep(t, s)

            sp.wait_ge(ones_ready, 7)
            for s in range(STREAMS):
                graph_load(0, s)
            for s in range(STREAMS):
                graph_load(1, s)
                graph_steps(0, s)
            with sp.Fori(2, NT) as t:
                for s in range(STREAMS):
                    graph_load(t, s)
                    graph_steps(t - 1, s)
                    store(t - 2, ATTN_ITS + t - 2, s, out)
            for s in range(STREAMS):
                graph_steps(NT - 1, s)
                store(NT - 2, ATTN_ITS + NT - 2, s, out)
            for s in range(STREAMS):
                store(NT - 1, ATTN_ITS + NT - 1, s, out)
            for s in range(STREAMS):
                sp.wait_ge(stored[s], (ATTN_ITS + NT) * 16 + 16)

        @block.gpsimd
        def _(pool):
            credit(pool, mask_ready, x_keep_ready, keep_ready, x_done)
            pool.memset(ident[:], 0.0).then_inc(const_ready, 1)
            pool.wait_ge(const_ready, 1)
            pool.affine_select(out=ident[:], in_=ident[:], compare_op=ALU.not_equal, fill=1.0, base=0,
                               pattern=[[-1, P]], channel_multiplier=1).then_inc(const_ready, 1)
            pool.wait_ge(const_ready, 2)
            pool.tensor_copy(ident_bf[:], ident[:]).then_inc(const_ready, 1)
            pool.memset(tail_w[:], 0.0).then_inc(const_ready, 1)
            pool.memset(head_ones[:], 0.0).then_inc(const_ready, 1)
            pool.wait_ge(const_ready, 5)
            for r in range(P // DK):
                pool.memset(head_ones[r * DK:(r + 1) * DK, r * DK:(r + 1) * DK], 1.0).then_inc(const_ready, 1)
                pool.wait_ge(const_ready, 6 + r)

            def mask_term(it, s):
                landed, freed = it * 16 + 16, it + FREED
                pool.compute_val(landed)
                pool.compute_val(freed)
                pool.wait_ge(const_ready, 9)
                pool.wait_ge(mask_loaded[s], landed)
                pool.wait_ge(scores_psum[GB - 1][s], freed)
                pool.tensor_scalar(mask_add[s][:], mask_raw[s], -1.0, MASKED, ALU.add, ALU.mult) \
                    .then_inc(mask_ready[s], 1)

            def add_bias(it, s, layer):
                pool.wait_ge(raw_loaded, layer * 32 + 32)
                pool.wait_ge(loaded[s], it * 16 + 16)
                pool.wait_ge(y_ready[s], it + FREED)
                pool.tensor_tensor(x_keep[s][:].rearrange("p (b f) -> p b f", b=GB), stage[s][:],
                                   bias_rows[:].unsqueeze(1).to_broadcast([P, GB, D]), ALU.add) \
                    .then_inc(x_keep_ready[s], 1)

            def norm_rows(it, s):
                full, unstored = it + FULL, it * 16 + 16
                pool.compute_val(full)
                pool.compute_val(unstored)
                pool.wait_ge(const_ready, 9)
                pool.wait_ge(rstd_ready[s], full)
                pool.wait_ge(stored[s], unstored)
                for b in range(GB):
                    last = pool.tensor_scalar(x_new[s][:, b * D:(b + 1) * D], y_sum[s][:, b * D:(b + 1) * D],
                                              mean_var[s][:, b, 0:1], rstd[s][:, b:b + 1], ALU.subtract, ALU.mult)
                last.then_inc(x_done[s], 1)

            def attention(before, now, nxt, layer):
                for s, other, summed in ((0, 1, before), (1, 0, now)):
                    if nxt is not None:
                        mask_term(nxt, s)
                    if summed is not None:
                        norm_rows(summed, other)
                    if nxt is not None:
                        add_bias(nxt, s, layer)

            with pool.Fori(0, LAYERS) as layer:
                first = layer * NT
                attention(None, None, first, layer)
                attention(None, first, first + 1, layer)
                with pool.Fori(1, NT - 1) as t:
                    attention(first + t - 1, first + t, first + t + 1, layer)
                attention(first + (NT - 2), first + (NT - 1), None, layer)
                norm_rows(first + (NT - 1), 1)

            with pool.Fori(0, NT) as t:
                landed = t * 16 + (ATTN_ITS * 16 + 16)
                summed = t + (ATTN_ITS + FREED)
                added = t * 2 + FREED
                for count in (landed, summed, added):
                    pool.compute_val(count)
                for s in range(STREAMS):
                    pool.wait_ge(const_ready, 9)
                    pool.wait_ge(mask_loaded[s], landed)
                    pool.wait_ge(y_ready[s], summed)
                    pool.tensor_scalar(keep[s][:], mask_raw[s][:, :, 0:1], -1.0, 1.0, ALU.mult, ALU.add) \
                        .then_inc(keep_ready[s], 1)
                    pool.wait_ge(scores_psum[GB - 1][s], ATTN_ITS + FREED)
                    pool.wait_ge(g_scores_psum[s], added)
                    pool.tensor_scalar(mask_add[s][:], mask_raw[s], -MASKED, 0.0, ALU.mult, ALU.add) \
                        .then_inc(mask_ready[s], 1)

        @block.tensor
        def _(pe):
            credit(pe, xt_psum, v_psum, *scores_psum, *pt_psum, o_psum, wo_psum, g_scores_psum, g_cos_psum, *gt_psum)
            credit(pe, q_psum, k_psum, m_psum, ss_psum, g_out_psum)

            def split_product(dst, left, right):
                n = len(SPLIT_PRODUCTS) * DC
                for i, (a, b) in enumerate(SPLIT_PRODUCTS):
                    for c in range(DC):
                        k = i * DC + c
                        last = pe.matmul(dst, left[a](c), right[b](c), start=(k == 0), stop=(k == n - 1))
                return last

            def transpose_rows(s, bank, rows):
                for b in range(GB):
                    for c in range(DC):
                        o = c * GB * N + b * N
                        last = pe.transpose(psum[s][:, bank, o:o + N], rows[:, b, c * P:(c + 1) * P], ident[:])
                return last

            def project_t(s, bank, slot):
                for m in range(DC):
                    last = split_product(
                        psum[s][:, bank, m * GB * N:(m + 1) * GB * N],
                        [lambda c, w=w: w[:, slot, c, m * P:(m + 1) * P] for w in w_part],
                        [lambda c, v=v: v[:, c, :] for v in xt[s]])
                return last

            def project_rows(s, bank, left, slot):
                for b in range(GB):
                    last = split_product(
                        psum[s][:, bank, b * D:(b + 1) * D],
                        [lambda c, v=v: v[:, c, b * N:(b + 1) * N] for v in left],
                        [lambda c, w=w: w[:, slot, c, :] for w in w_part])
                return last

            def transpose_x(it, s):
                pe.wait_ge(loaded[s], it * 16 + 16)
                transpose_rows(s, SC1, stage[s]).then_inc(xt_psum[s], 1)

            def project_qk(it, s, layer):
                pe.wait_ge(w_split, layer + 1)
                pe.wait_ge(xt_hi_ready[s], it + FULL)
                pe.wait_ge(xt_lo_ready[s], it + FULL)
                project_t(s, WK1, WQ).then_inc(q_psum[s], 1)
                project_t(s, WK0, WK).then_inc(k_psum[s], 1)

            def project_v(it, s):
                pe.wait_ge(ot_hi_ready[s], it + FREED)
                pe.wait_ge(ot_lo_ready[s], it + FREED)
                project_rows(s, SC0, xt[s], WV).then_inc(v_psum[s], 1)

            def scores(it, s):
                pe.wait_ge(mask_ready[s], it + FULL)
                pe.wait_ge(q_hi_ready[s], it + FULL)
                pe.wait_ge(q_lo_ready[s], it + FULL)
                pe.wait_ge(k_hi_ready[s], it + FULL)
                pe.wait_ge(k_lo_ready[s], it + FULL)
                for b in range(GB):
                    if b == 0:
                        pe.wait_ge(v_ready[s], it + FULL)
                    else:
                        pe.wait_ge(y_ready[s], it + FREED)
                    pe.matmul(psum[s][:, SC0 + b, :].rearrange("p (h j) -> p h j", h=H), ident_bf[:],
                              mask_add[s][:, b, :].unsqueeze(1).to_broadcast([P, H, N]), start=True, stop=True)
                    for left, right in SPLIT_PRODUCTS:
                        for c in range(DC):
                            last = pe.matmul(psum[s][:, SC0 + b, c * 2 * N:(c + 1) * 2 * N]
                                             .rearrange("p (r j) -> p r j", r=2),
                                             k_part[s][:, left, c, b], pair_diag[s][:, :, right, c, b],
                                             start=False, stop=True, skip_group_check=True)
                    last.then_inc(scores_psum[b][s], 1)

            def transpose_probs(it, s):
                for b in range(GB):
                    pe.wait_ge(probs_ready[b][s], it + FULL)
                    for h in range(H):
                        last = pe.transpose(psum[s][:, WK0 + b, h * N:(h + 1) * N], probs[s][:, b, h, :], ident[:])
                    last.then_inc(pt_psum[b][s], 1)

            def weighted_values(it, s):
                for b in range(GB):
                    pe.wait_ge(pt_ready[b][s], it + FULL)
                    for h in range(H):
                        c, r = divmod(h, 2)
                        o = c * GB * N + b * N
                        last = pe.matmul(psum[s][r * DH:(r + 1) * DH, SC0, o:o + N],
                                         v_rows[s][:, b * D + h * DH:b * D + (h + 1) * DH], probs_t[s][:, b, h, :],
                                         start=True, stop=True)
                last.then_inc(o_psum[s], 1)

            def project_out(it, s):
                pe.wait_ge(ot_hi_ready[s], it + FULL)
                pe.wait_ge(ot_lo_ready[s], it + FULL)
                project_rows(s, SC1, ot[s], WO).then_inc(wo_psum[s], 1)

            def attention(now, nxt, layer):
                for s, other, ending in ((0, 1, now), (1, 0, nxt)):
                    if nxt is not None:
                        transpose_x(nxt, s)
                    if ending is not None:
                        scores(ending, other)
                    if now is not None:
                        weighted_values(now, s)
                    if nxt is not None:
                        project_qk(nxt, s, layer)
                    if now is not None:
                        project_out(now, s)
                    if nxt is not None:
                        project_v(nxt, s)
                    if ending is not None:
                        transpose_probs(ending, other)

            def fuse_weights():
                bank = psum[0]
                pe.wait_ge(graph_raw_loaded, 16 * 7)
                pe.wait_ge(gb_wide_ready, 1)
                for i in range(2):
                    for m in range(DC):
                        for c in range(DC):
                            pe.matmul(bank[:, i, m * D:(m + 1) * D], raw_w[:, RAW_M, c, m * P:(m + 1) * P],
                                      raw_w[:, RAW_QT + i, c, :], start=(c == 0), stop=(c == DC - 1))
                for m in range(DC):
                    for c in range(DC):
                        o = m * D + c * P
                        pe.matmul(bank[:, 2, o:o + P], raw_g[:, c, m * P:(m + 1) * P], tail_w[:], start=True, stop=True)
                for i in range(2):
                    for m in range(DC):
                        for c in range(DC):
                            pe.matmul(bank[:, 3, i * DC + m:i * DC + m + 1], raw_w[:, RAW_QT + i, c, m * P:(m + 1) * P],
                                      cols[:, 0, c:c + 1], start=(c == 0), stop=(c == DC - 1))
                for c in range(DC):
                    last = pe.matmul(bank[:, 3, P + c * P:P + (c + 1) * P], gb_wide[:, c, :], tail_w[:],
                                     start=True, stop=True)
                last.then_inc(fused_psum, 1)

            def graph_transpose_x(t, s):
                pe.wait_ge(loaded[s], (ATTN_ITS + t) * 16 + 16)
                transpose_rows(s, 3, stage[s]).then_inc(xt_psum[s], 1)

            def graph_projections(t, s):
                pe.wait_ge(xt_hi_ready[s], ATTN_ITS + t + FULL)
                pe.wait_ge(xt_lo_ready[s], ATTN_ITS + t + FULL)
                project_t(s, 3, WM).then_inc(m_psum[s], 1)
                project_t(s, 0, WMQ).then_inc(q_psum[s], 1)
                project_t(s, 1, WMK).then_inc(k_psum[s], 1)

            def square_sums(t, s):
                pe.wait_ge(y_ready[s], ATTN_ITS + t + FREED)
                pe.wait_ge(sq_ready[s], t + FULL)
                for c in range(DC):
                    last = pe.matmul(psum[s][:, 2, c * GB * N:(c + 1) * GB * N], head_ones[:], kt[s][:, c, :],
                                     start=True, stop=True)
                last.then_inc(ss_psum[s], 1)

            def graph_values(t, s):
                pe.wait_ge(m_ready[s], t + FULL)
                project_rows(s, 3, xt[s], WG).then_inc(v_psum[s], 1)

            def graph_scores(t, s, half):
                if half == 0:
                    pe.wait_ge(mask_ready[s], ATTN_ITS + t + FULL)
                    pe.wait_ge(q_hi_ready[s], ATTN_ITS + t + FULL)
                    pe.wait_ge(q_lo_ready[s], ATTN_ITS + t + FULL)
                    pe.wait_ge(k_spread[s], t * 64 + 64)
                for b in range(GB):
                    pe.matmul(psum[s][:, b, :].rearrange("p (r j) -> p r j", r=4), ident_bf[:],
                              mask_add[s][:, b, :].unsqueeze(1).to_broadcast([P, 4, N]), start=True, stop=True)
                    for left, right in SPLIT_PRODUCTS:
                        last = pe.matmul(psum[s][:, b, :].rearrange("p (r j) -> p r j", r=4), ot[s][left][:, half, b * N:(b + 1) * N],
                                         k_diag[s][:, :, right, half, b],
                                         start=False, stop=True, skip_group_check=True)
                last.then_inc(g_scores_psum[s], 1)

            def graph_cosines(t, s, half):
                if half == 0:
                    pe.wait_ge(n_spread[s], t * 64 + 64)
                    order = ((0, None), (1, v_ready[s]))
                    free_count = ATTN_ITS + t + FULL
                else:
                    order = ((1, None), (0, half_ready[s]))
                    free_count = t + FULL
                for b, bank_free in order:
                    if bank_free is not None:
                        pe.wait_ge(bank_free, free_count)
                    for i, (left, right) in enumerate(SPLIT_PRODUCTS):
                        last = pe.matmul(psum[s][:, 2 + b, :].rearrange("p (r j) -> p r j", r=4), n_part[s][:, left, half, b],
                                         n_diag[s][:, :, right, half, b],
                                         start=(i == 0), stop=(i == len(SPLIT_PRODUCTS) - 1))
                last.then_inc(g_cos_psum[s], 1)

            def transpose_gates(t, s, half):
                for b in range(GB):
                    pe.wait_ge(gate_ready[b][s], t * 2 + half + FULL)
                    for r in range(4):
                        last = pe.transpose(psum[s][:, b, r * N:(r + 1) * N], probs[s][:, b, r, :], ident[:])
                    last.then_inc(gt_psum[b][s], 1)

            def gated_values(t, s, half):
                for b in range(GB):
                    pe.wait_ge(gt_ready[b][s], t * 2 + half + FULL)
                    for r in range(4):
                        o = (b * 4 + r) * (DK + 1)
                        last = pe.matmul(psum[s][:, 2, o:o + DK + 1], probs_t[s][:, b, r, :],
                                         g_ones[s][:, b, 4 * half + r, :], start=True, stop=True)
                last.then_inc(g_out_psum[s], 1)

            def graph(now, nxt):
                for s, other, ending in ((0, 1, now), (1, 0, nxt)):
                    if nxt is not None:
                        graph_transpose_x(nxt, s)
                    if now is not None:
                        gated_values(now, s, 1)
                    if nxt is not None:
                        graph_projections(nxt, s)
                        square_sums(nxt, s)
                    if ending is not None:
                        transpose_gates(ending, other, 0)
                    if nxt is not None:
                        graph_values(nxt, s)
                    if ending is not None:
                        gated_values(ending, other, 0)
                        graph_scores(ending, other, 1)
                        graph_cosines(ending, other, 1)
                    if nxt is not None:
                        graph_scores(nxt, s, 0)
                        graph_cosines(nxt, s, 0)
                    if ending is not None:
                        transpose_gates(ending, other, 1)

            pe.wait_ge(const_ready, 9)
            with pe.Fori(0, LAYERS) as layer:
                first = layer * NT
                for s in range(STREAMS):
                    pe.wait_ge(y_ready[s], first + FREED)
                attention(None, first, layer)
                with pe.Fori(0, NT - 1) as t:
                    attention(first + t, first + t + 1, layer)
                attention(first + (NT - 1), None, layer)

            for s in range(STREAMS):
                pe.wait_ge(y_ready[s], ATTN_ITS + FREED)
            fuse_weights()
            pe.wait_ge(fused_ready, 1)
            graph(None, 0)
            with pe.Fori(0, NT - 1) as t:
                graph(t, t + 1)
            graph(NT - 1, None)

        @block.scalar
        def _(act):
            credit(act, xt_hi_ready, v_ready, *exp_ready, pt_ready[1], ot_hi_ready, log_ready, rstd_ready,
                   m_ready, sq_ready, ss_log_ready, inv_norm_ready, q_hi_ready, k_hi_ready, n_hi_ready,
                   *g_exp_ready, gt_ready[1])

            def split_hi(it, s, bank):
                act.wait_ge(xt_psum[s], it + FULL)
                act.wait_ge(v_psum[s], it + FREED)
                act.activation(xt[s][HI][:].rearrange("p c n -> p (c n)"), psum[s][:, bank, :], ACT.Copy) \
                   .then_inc(xt_hi_ready[s], 1)

            def q_hi(it, s):
                act.wait_ge(q_psum[s], it + FULL)
                act.activation(k_part[s][:, HI].rearrange("p c b n -> p (c b n)"), psum[s][:, WK1, :], ACT.Copy,
                               scale=float(DH) ** -0.5).then_inc(q_hi_ready[s], 1)

            def k_hi(it, s):
                act.wait_ge(k_psum[s], it + FULL)
                for r in range(2):
                    rows = slice(r * DH, (r + 1) * DH)
                    last = act.activation(pair_diag[s][rows, r, HI].rearrange("p c b n -> p (c b n)"),
                                          psum[s][rows, WK0, :], ACT.Copy)
                last.then_inc(k_hi_ready[s], 1)

            def v_out(it, s):
                act.wait_ge(v_psum[s], it + FULL)
                act.wait_ge(o_psum[s], it + FREED)
                act.activation(v_rows[s], psum[s][:, SC0, :], ACT.Copy).then_inc(v_ready[s], 1)

            def exps(it, s, b):
                act.wait_ge(max_ready[b][s], it + FULL)
                act.wait_ge(pt_psum[b][s], it + FREED)
                for h in range(H):
                    last = act.activation(probs[s][:, b, h, :], psum[s][:, SC0 + b, h * N:(h + 1) * N], ACT.Exp,
                                          bias=neg_max[s][:, b * H + h:b * H + h + 1],
                                          accum_out=row_sum[s][:, b, h:h + 1])
                last.then_inc(exp_ready[b][s], 1)

            def pt1(it, s):
                act.wait_ge(pt_psum[1][s], it + FULL)
                act.activation(probs_t[s][:, 1].rearrange("p h i -> p (h i)"), psum[s][:, WK1, :], ACT.Copy) \
                   .then_inc(pt_ready[1][s], 1)

            def ot_hi(it, s):
                act.wait_ge(o_psum[s], it + FULL)
                act.wait_ge(wo_psum[s], it + FREED)
                act.activation(ot[s][HI][:].rearrange("p c n -> p (c n)"), psum[s][:, SC0, :], ACT.Copy) \
                   .then_inc(ot_hi_ready[s], 1)

            def rstd_of(it, s):
                act.wait_ge(mv_ready[s], it + FULL)
                act.activation(log_var[s][:], mean_var[s][:, :, 1], ACT.Ln, bias=eps_col[:, 0:1]) \
                   .then_inc(log_ready[s], 1)
                act.wait_ge(log_ready[s], it + FULL)
                act.activation(rstd[s][:], log_var[s][:], ACT.Exp, scale=-0.5).then_inc(rstd_ready[s], 1)

            def attention(before, now, nxt):
                for s, other, ending, summed in ((0, 1, now, before), (1, 0, nxt, now)):
                    if now is not None:
                        pt1(now, s)
                    if nxt is not None:
                        split_hi(nxt, s, SC1)
                    if ending is not None:
                        exps(ending, other, 0)
                    if now is not None:
                        ot_hi(now, s)
                    if ending is not None:
                        exps(ending, other, 1)
                    if nxt is not None:
                        q_hi(nxt, s)
                        k_hi(nxt, s)
                    if summed is not None:
                        rstd_of(summed, other)
                    if nxt is not None:
                        v_out(nxt, s)

            def m_out(t, s):
                act.wait_ge(m_psum[s], t + FULL)
                act.wait_ge(n_lo_ready[s], t + FREED)
                for c in range(DC):
                    last = act.activation(qt[s][:, c, :], psum[s][:, 3, c * GB * N:(c + 1) * GB * N], ACT.Identity,
                                          bias=cols[:, 0, c:c + 1])
                last.then_inc(m_ready[s], 1)
                act.wait_ge(m_ready[s], t + FULL)
                act.wait_ge(n_ready[s], t + FREED)
                act.activation(flat["sq"][s], flat["m"][s], ACT.Square).then_inc(sq_ready[s], 1)

            def graph_q_hi(t, s):
                act.wait_ge(q_psum[s], ATTN_ITS + t + FULL)
                act.wait_ge(g_scores_psum[s], t * 2 + FREED)
                for c in range(DC):
                    last = act.activation(ot[s][HI][:, c, :], psum[s][:, 0, c * GB * N:(c + 1) * GB * N], ACT.Identity,
                                          bias=fused_b[:, 0, c:c + 1])
                last.then_inc(q_hi_ready[s], 1)

            def graph_k_hi(t, s):
                act.wait_ge(k_psum[s], ATTN_ITS + t + FULL)
                act.wait_ge(g_scores_psum[s], t * 2 + FREED)
                for c in range(DC):
                    last = act.activation(k_part[s][:, HI, c].rearrange("p b n -> p (b n)"),
                                          psum[s][:, 1, c * GB * N:(c + 1) * GB * N], ACT.Identity,
                                          bias=fused_b[:, 1, c:c + 1])
                last.then_inc(k_hi_ready[s], 1)

            def inverse_norms(t, s):
                act.wait_ge(ss_ready[s], t + FULL)
                act.activation(flat["sq"][s], flat["sq"][s], ACT.Ln).then_inc(ss_log_ready[s], 1)
                act.wait_ge(ss_log_ready[s], t + FULL)
                act.activation(flat["sq"][s], flat["sq"][s], ACT.Exp, scale=-0.5).then_inc(inv_norm_ready[s], 1)

            def n_hi(t, s):
                act.wait_ge(n_ready[s], t + FULL)
                act.wait_ge(g_cos_psum[s], t * 2 + FREED)
                act.activation(n_part[s][:, HI].rearrange("p c b n -> p (c b n)"), flat["m"][s], ACT.Copy) \
                   .then_inc(n_hi_ready[s], 1)

            def graph_exps(t, s, half, b):
                act.wait_ge(g_max_ready[b][s], t * 2 + half + FULL)
                if half == 0:
                    act.wait_ge(y_ready[s], ATTN_ITS + t + FREED)
                else:
                    act.wait_ge(gt_psum[b][s], t * 2 + half + FREED)
                for r in range(4):
                    h = 4 * half + r
                    last = act.activation(probs[s][:, b, r, :], psum[s][:, b, r * N:(r + 1) * N], ACT.Exp,
                                          bias=neg_max[s][:, b * 4 + r:b * 4 + r + 1],
                                          accum_out=row_sum[s][:, b, h:h + 1])
                last.then_inc(g_exp_ready[b][s], 1)

            def gt1(t, s, half):
                act.wait_ge(gt_psum[1][s], t * 2 + half + FULL)
                act.activation(probs_t[s][:, 1].rearrange("p r i -> p (r i)"), psum[s][:, 1, :], ACT.Copy) \
                   .then_inc(gt_ready[1][s], 1)

            def graph(now, nxt):
                for s, other, ending in ((0, 1, now), (1, 0, nxt)):
                    if ending is not None:
                        graph_exps(ending, other, 0, 0)
                    if now is not None:
                        gt1(now, s, 1)
                    if nxt is not None:
                        split_hi(ATTN_ITS + nxt, s, 3)
                    if ending is not None:
                        graph_exps(ending, other, 0, 1)
                    if nxt is not None:
                        m_out(nxt, s)
                        graph_q_hi(nxt, s)
                        graph_k_hi(nxt, s)
                        inverse_norms(nxt, s)
                    if ending is not None:
                        gt1(ending, other, 0)
                    if nxt is not None:
                        n_hi(nxt, s)
                    if now is not None:
                        rstd_of(ATTN_ITS + now, s)
                    if ending is not None:
                        graph_exps(ending, other, 1, 0)
                        graph_exps(ending, other, 1, 1)

            act.preload_act_table_set("natural_log_exp_and_others")
            act.wait_ge(ones_ready, 7)
            with act.Fori(0, LAYERS) as layer:
                first = layer * NT
                attention(None, None, first)
                attention(None, first, first + 1)
                with act.Fori(1, NT - 1) as t:
                    attention(first + t - 1, first + t, first + t + 1)
                attention(first + (NT - 2), first + (NT - 1), None)
                rstd_of(first + (NT - 1), 1)
            act.wait_ge(graph_raw_loaded, 16 * 7)
            graph(None, 0)
            with act.Fori(0, NT - 1) as t:
                graph(t, t + 1)
            graph(NT - 1, None)

        @block.vector
        def _(dve):
            credit(dve, xt_lo_ready, *max_ready, *rcp_ready, *probs_ready, pt_ready[0], ot_lo_ready, y_ready, bn_ready,
                   mv_ready, ss_ready, n_ready, q_lo_ready, k_lo_ready, n_lo_ready, *g_max_ready,
                   *gate_ready, gt_ready[0], half_ready, total_ready, g_rcp_ready, g_scale_ready, scaled_ready)

            def split_lo(it, s, bank):
                dve.wait_ge(xt_hi_ready[s], it + FULL)
                dve.tensor_tensor(xt[s][LO][:].rearrange("p c n -> p (c n)"), psum[s][:, bank, :],
                                  xt[s][HI][:].rearrange("p c n -> p (c n)").bitcast(F32), ALU.subtract) \
                   .then_inc(xt_lo_ready[s], 1)

            def q_lo(it, s):
                dve.wait_ge(q_hi_ready[s], it + FULL)
                dve.scalar_tensor_tensor(k_part[s][:, LO].rearrange("p c b n -> p (c b n)"), psum[s][:, WK1, :],
                                         float(DH) ** -0.5, k_part[s][:, HI].rearrange("p c b n -> p (c b n)")
                                         .bitcast(F32), ALU.mult, ALU.subtract).then_inc(q_lo_ready[s], 1)

            def k_lo(it, s):
                dve.wait_ge(k_hi_ready[s], it + FULL)
                for r in range(2):
                    rows = slice(r * DH, (r + 1) * DH)
                    last = dve.tensor_tensor(pair_diag[s][rows, r, LO].rearrange("p c b n -> p (c b n)"),
                                             psum[s][rows, WK0, :],
                                             pair_diag[s][rows, r, HI].rearrange("p c b n -> p (c b n)").bitcast(F32),
                                             ALU.subtract)
                last.then_inc(k_lo_ready[s], 1)

            def maxima(it, s, b):
                dve.wait_ge(scores_psum[b][s], it + FULL)
                dve.wait_ge(exp_ready[b][s], it + FREED)
                dve.tensor_reduce(neg_max[s][:, b * H:(b + 1) * H],
                                  psum[s][:, SC0 + b, :].rearrange("p (h j) -> p h j", h=H),
                                  AX_X, ALU.max, negate=True).then_inc(max_ready[b][s], 1)

            def normalise(it, s, b):
                r = rcp[s][:, b * H:(b + 1) * H]
                dve.wait_ge(exp_ready[b][s], it + FULL)
                dve.reciprocal(r, row_sum[s][:, b, 0:H]).then_inc(rcp_ready[b][s], 1)
                dve.wait_ge(rcp_ready[b][s], it + FULL)
                dve.tensor_tensor(probs[s][:, b], probs[s][:, b], r.unsqueeze(2).to_broadcast([P, H, N]), ALU.mult) \
                   .then_inc(probs_ready[b][s], 1)

            def pt0(it, s):
                dve.wait_ge(pt_psum[0][s], it + FULL)
                dve.tensor_copy(probs_t[s][:, 0].rearrange("p h i -> p (h i)"), psum[s][:, WK0, :]) \
                   .then_inc(pt_ready[0][s], 1)

            def ot_lo(it, s):
                dve.wait_ge(ot_hi_ready[s], it + FULL)
                dve.tensor_tensor(ot[s][LO][:].rearrange("p c n -> p (c n)"), psum[s][:, SC0, :],
                                  ot[s][HI][:].rearrange("p c n -> p (c n)").bitcast(F32), ALU.subtract) \
                   .then_inc(ot_lo_ready[s], 1)

            def residual(it, s):
                dve.wait_ge(wo_psum[s], it + FULL)
                dve.wait_ge(x_keep_ready[s], it + FULL)
                dve.wait_ge(x_done[s], it + FREED)
                dve.tensor_tensor(y_sum[s][:], psum[s][:, SC1, :], x_keep[s][:], ALU.add).then_inc(y_ready[s], 1)

            def statistics(it, s):
                dve.wait_ge(y_ready[s], it + FULL)
                for b in range(GB):
                    last = dve.bn_stats(bn[s][:, b, :], y_sum[s][:, b * D:(b + 1) * D])
                last.then_inc(bn_ready[s], 1)
                dve.wait_ge(ones_ready, 7)
                dve.wait_ge(bn_ready[s], it + FULL)
                for b in range(GB):
                    last = dve.bn_aggr(mean_var[s][:, b, :], bn[s][:, b, :])
                last.then_inc(mv_ready[s], 1)

            def norm_rows(it, s):
                dve.wait_ge(rstd_ready[s], it + FULL)
                dve.wait_ge(stored[s], it * 16 + 16)
                for b in range(GB):
                    last = dve.tensor_scalar(x_new[s][:, b * D:(b + 1) * D], y_sum[s][:, b * D:(b + 1) * D],
                                             mean_var[s][:, b, 0:1], rstd[s][:, b:b + 1], ALU.subtract, ALU.mult)
                last.then_inc(x_done[s], 1)

            def attention(before, now, nxt):
                for s, other, ending, summed in ((0, 1, now, before), (1, 0, nxt, now)):
                    if now is not None:
                        pt0(now, s)
                    if nxt is not None:
                        split_lo(nxt, s, SC1)
                    if ending is not None:
                        maxima(ending, other, 0)
                        maxima(ending, other, 1)
                    if summed is not None:
                        statistics(summed, other)
                    if ending is not None:
                        normalise(ending, other, 0)
                    if now is not None:
                        ot_lo(now, s)
                    if ending is not None:
                        normalise(ending, other, 1)
                    if nxt is not None:
                        q_lo(nxt, s)
                        k_lo(nxt, s)
                    if now is not None:
                        residual(now, s)

            def split_fused():
                bank = psum[0]
                dve.wait_ge(fused_psum, 1)
                flat_w = [w[:].rearrange("p m c o -> p m (c o)") for w in w_part]
                dve.tensor_copy(flat_w[HI][:, WM, :], raw_w[:, RAW_MT].rearrange("p c o -> p (c o)"))
                dve.tensor_scalar(flat_w[HI][:, WMQ, :], bank[:, 0, :], GSCALE, None, ALU.mult)
                dve.tensor_copy(flat_w[HI][:, WMK:WG + 1, :], bank[:, 1:3, :]).then_inc(fused_hi_ready, 1)
                for c in range(DC):
                    dve.tensor_scalar(fused_b[:, 0, c:c + 1], bank[:, 3, c:c + 1], cols[:, 1, c:c + 1], GSCALE,
                                      ALU.add, ALU.mult)
                dve.tensor_tensor(fused_b[:, 1, :], bank[:, 3, DC:2 * DC], cols[:, 2, :], ALU.add)
                dve.tensor_copy(bias_rows[:], bank[:, 3, P:P + D])
                dve.wait_ge(fused_hi_ready, 1)
                dve.tensor_tensor(flat_w[LO][:, WM, :], raw_w[:, RAW_MT].rearrange("p c o -> p (c o)"),
                                  flat_w[HI][:, WM, :].bitcast(F32), ALU.subtract)
                dve.scalar_tensor_tensor(flat_w[LO][:, WMQ, :], bank[:, 0, :], GSCALE,
                                         flat_w[HI][:, WMQ, :].bitcast(F32), ALU.mult, ALU.subtract)
                dve.tensor_tensor(flat_w[LO][:, WMK:WG + 1, :], bank[:, 1:3, :],
                                  flat_w[HI][:, WMK:WG + 1, :].bitcast(F32), ALU.subtract)
                for s in range(STREAMS):
                    last = dve.memset(g_ones[s][:, :, :, DK:DK + 1], 1.0)
                last.then_inc(fused_ready, 1)
                dve.wait_ge(fused_ready, 1)

            def graph_q_lo(t, s):
                dve.wait_ge(q_hi_ready[s], ATTN_ITS + t + FULL)
                for c in range(DC):
                    last = dve.scalar_tensor_tensor(ot[s][LO][:, c, :], psum[s][:, 0, c * GB * N:(c + 1) * GB * N],
                                                    fused_b[:, 0, c:c + 1], ot[s][HI][:, c, :].bitcast(F32),
                                                    ALU.add, ALU.subtract)
                last.then_inc(q_lo_ready[s], 1)

            def graph_k_lo(t, s):
                dve.wait_ge(k_hi_ready[s], ATTN_ITS + t + FULL)
                for c in range(DC):
                    last = dve.scalar_tensor_tensor(k_part[s][:, LO, c].rearrange("p b n -> p (b n)"),
                                                    psum[s][:, 1, c * GB * N:(c + 1) * GB * N], fused_b[:, 1, c:c + 1],
                                                    k_part[s][:, HI, c].rearrange("p b n -> p (b n)").bitcast(F32),
                                                    ALU.add, ALU.subtract)
                last.then_inc(k_lo_ready[s], 1)

            def norm_guard(t, s):
                dve.wait_ge(ss_psum[s], t + FULL)
                dve.tensor_scalar(flat["sq"][s], psum[s][:, 2, :], NORM2_MIN, None, ALU.max).then_inc(ss_ready[s], 1)

            def normalised(t, s):
                dve.wait_ge(inv_norm_ready[s], t + FULL)
                dve.tensor_tensor(flat["m"][s], flat["m"][s], flat["sq"][s], ALU.mult).then_inc(n_ready[s], 1)

            def n_lo(t, s):
                dve.wait_ge(n_hi_ready[s], t + FULL)
                dve.tensor_tensor(n_part[s][:, LO].rearrange("p c b n -> p (c b n)"), flat["m"][s],
                                  n_part[s][:, HI].rearrange("p c b n -> p (c b n)").bitcast(F32), ALU.subtract) \
                   .then_inc(n_lo_ready[s], 1)

            def graph_v(t, s):
                dve.wait_ge(v_psum[s], ATTN_ITS + t + FULL)
                dve.wait_ge(g_out_psum[s], t * 2 + FREED)
                dve.tensor_tensor(g_ones[s][:, :, :, 0:DK],
                                  psum[s][:, 3, :].rearrange("p (b h d) -> p b h d", b=GB, h=GH),
                                  bias_rows[:].rearrange("p (h d) -> p h d", h=GH).unsqueeze(1)
                                  .to_broadcast([P, GB, GH, DK]), ALU.add).then_inc(v_ready[s], 1)

            def graph_maxima(t, s, half, b):
                dve.wait_ge(g_scores_psum[s], t * 2 + half + FULL)
                dve.wait_ge(g_exp_ready[b][s], t * 2 + half + FREED)
                dve.tensor_reduce(neg_max[s][:, b * 4:(b + 1) * 4], psum[s][:, b, :].rearrange("p (r j) -> p r j", r=4),
                                  AX_X, ALU.max, negate=True).then_inc(g_max_ready[b][s], 1)

            def gate(t, s, half, b):
                e = probs[s][:, b].rearrange("p r j -> p (r j)")
                dve.wait_ge(g_exp_ready[b][s], t * 2 + half + FULL)
                dve.wait_ge(g_cos_psum[s], t * 2 + half + FULL)
                dve.scalar_tensor_tensor(e, psum[s][:, 2 + b, :], THRESHOLD, e, ALU.is_gt, ALU.mult) \
                   .then_inc(gate_ready[b][s], 1)

            def gt0(t, s, half):
                dve.wait_ge(gt_psum[0][s], t * 2 + half + FULL)
                dve.tensor_copy(probs_t[s][:, 0].rearrange("p r i -> p (r i)"), psum[s][:, 0, :]) \
                   .then_inc(gt_ready[0][s], 1)

            HALF = GB * 4 * (DK + 1)

            def first_half(t, s):
                dve.wait_ge(g_out_psum[s], t * 2 + FULL)
                dve.tensor_copy(half_out[s][:], psum[s][:, 2, 0:HALF]).then_inc(half_ready[s], 1)

            def graph_output(t, s):
                halves = [h.rearrange("p (b r d) -> p b r d", b=GB, r=4)
                          for h in (half_out[s][:], psum[s][:, 2, 0:HALF])]
                tot = total[s][:].rearrange("p (b h) -> p b h", b=GB)
                inv = rcp[s][:].rearrange("p (b h) -> p b h", b=GB)
                scaled = probs_all[:, s, 0:GF].rearrange("p (b h d) -> p b h d", b=GB, h=GH)
                dve.wait_ge(g_out_psum[s], t * 2 + 1 + FULL)
                dve.wait_ge(half_ready[s], t + FULL)
                for i in range(2):
                    last = dve.tensor_tensor(tot[:, :, 4 * i:4 * i + 4], halves[i][:, :, :, DK],
                                             row_sum[s][:, :, 4 * i:4 * i + 4], ALU.add)
                last.then_inc(total_ready[s], 1)
                dve.wait_ge(total_ready[s], t + FULL)
                dve.reciprocal(rcp[s][:], total[s][:]).then_inc(g_rcp_ready[s], 1)
                dve.wait_ge(g_rcp_ready[s], t + FULL)
                dve.wait_ge(keep_ready[s], t + FULL)
                dve.tensor_tensor(tot, inv, keep[s][:].to_broadcast([P, GB, GH]), ALU.mult).then_inc(g_scale_ready[s], 1)
                dve.wait_ge(g_scale_ready[s], t + FULL)
                for i in range(2):
                    last = dve.tensor_tensor(scaled[:, :, 4 * i:4 * i + 4, :], halves[i][:, :, :, 0:DK],
                                             tot[:, :, 4 * i:4 * i + 4].unsqueeze(3).to_broadcast([P, GB, 4, DK]),
                                             ALU.mult)
                last.then_inc(scaled_ready[s], 1)
                dve.wait_ge(scaled_ready[s], t + FULL)
                dve.wait_ge(kept[s], t * 16 + 16)
                dve.scalar_tensor_tensor(y_sum[s][:], probs_all[:, s, 0:GF], 0.0, x_keep[s][:], ALU.max, ALU.add) \
                   .then_inc(y_ready[s], 1)

            def graph(now, nxt):
                for s, other, ending in ((0, 1, now), (1, 0, nxt)):
                    if now is not None:
                        gt0(now, s, 1)
                    if ending is not None:
                        graph_maxima(ending, other, 0, 1)
                    if nxt is not None:
                        split_lo(ATTN_ITS + nxt, s, 3)
                    if ending is not None:
                        gate(ending, other, 0, 0)
                    if now is not None:
                        graph_output(now, s)
                    if ending is not None:
                        gate(ending, other, 0, 1)
                    if nxt is not None:
                        norm_guard(nxt, s)
                        graph_k_lo(nxt, s)
                    if ending is not None:
                        gt0(ending, other, 0)
                    if nxt is not None:
                        normalised(nxt, s)
                        graph_q_lo(nxt, s)
                        n_lo(nxt, s)
                    if ending is not None:
                        first_half(ending, other)
                    if now is not None:
                        statistics(ATTN_ITS + now, s)
                    if ending is not None:
                        graph_maxima(ending, other, 1, 0)
                        graph_maxima(ending, other, 1, 1)
                    if nxt is not None:
                        graph_v(nxt, s)
                    if ending is not None:
                        gate(ending, other, 1, 0)
                    if now is not None:
                        norm_rows(ATTN_ITS + now, s)
                    if nxt is not None:
                        graph_maxima(nxt, s, 0, 0)
                    if ending is not None:
                        gate(ending, other, 1, 1)

            dve.memset(eps_col[:], LN_EPS).then_inc(ones_ready, 1)
            for s in range(STREAMS):
                dve.memset(pair_diag[s][:].rearrange("p r w c b j -> p (r w c b j)").bitcast(F32), 0.0) \
                   .then_inc(ones_ready, 1)
            for s in range(STREAMS):
                for diag in (k_diag, n_diag):
                    dve.memset(diag[s][:].rearrange("p r w c b j -> p (r w c b j)").bitcast(F32), 0.0) \
                       .then_inc(ones_ready, 1)
            with dve.Fori(0, LAYERS) as layer:
                first = layer * NT
                dve.wait_ge(raw_loaded, layer * 32 + 32)
                for s in range(STREAMS):
                    dve.wait_ge(wo_psum[s], first + FREED)
                hi = w_part[HI][:].rearrange("p m c o -> p (m c o)")
                lo = w_part[LO][:].rearrange("p m c o -> p (m c o)")
                raw = raw_w.rearrange("p m c o -> p (m c o)")
                dve.tensor_copy(hi, raw).then_inc(w_hi_ready, 1)
                dve.wait_ge(w_hi_ready, layer + 1)
                dve.tensor_tensor(lo, raw, hi.bitcast(F32), ALU.subtract).then_inc(w_split, 1)
                attention(None, None, first)
                attention(None, first, first + 1)
                with dve.Fori(1, NT - 1) as t:
                    attention(first + t - 1, first + t, first + t + 1)
                attention(first + (NT - 2), first + (NT - 1), None)
                statistics(first + (NT - 1), 1)

            dve.wait_ge(graph_raw_loaded, 16 * 7)
            for c in range(DC):
                last = dve.tensor_copy(gb_wide[:, c, :], cols[:, 3, c:c + 1].to_broadcast([P, P]))
            last.then_inc(gb_wide_ready, 1)
            for s in range(STREAMS):
                dve.wait_ge(x_keep_ready[s], ATTN_ITS + FREED)
            split_fused()
            graph(None, 0)
            with dve.Fori(0, NT - 1) as t:
                graph(t, t + 1)
            graph(NT - 1, None)


def kernel(x, adj, **w):
    import numpy as np
    import concourse.bacc as bacc
    from concourse.bass_utils import run_bass_kernel_spmd

    def arr(name):
        return np.asarray(w[name])

    x = np.ascontiguousarray(np.asarray(x))
    D = x.shape[2]
    P = 128
    attn = range(3)
    arrays = {
        "x": x,
        "adj": np.ascontiguousarray(np.asarray(adj)).view(np.int32),
        "attn_w": np.stack([np.stack([arr(f"L{l}_gnn_{m}") for m in ("Wq", "Wk", "Wv", "Wo")]) for l in attn]),
        "attn_bo": np.ascontiguousarray(np.broadcast_to(np.stack([arr(f"L{l}_gnn_bo") for l in attn])[:, None], (3, P, D))),
        "gcn_w": np.stack([arr("L3_gnn_map_w").T, arr("L3_gnn_map_w"), arr("L3_gnn_q_w").T, arr("L3_gnn_k_w").T,
                           arr("L3_gnn_gcn_map_w")]),
        "gcn_cols": np.ascontiguousarray(np.stack([arr(f"L3_gnn_{b}") for b in ("map_b", "q_b", "k_b", "gcn_map_b")])
                                         .reshape(4, D // P, P).transpose(2, 0, 1)),
        "gcn_tail": np.ascontiguousarray(arr("L3_gnn_gcn_W").T),
    }
    nc = bacc.Bacc("TRN2", target_bir_lowering=False, num_devices=1)
    args = [nc.dram_tensor(f"in_{n}", a.shape, mybir.dt.from_np(a.dtype), kind="ExternalInput").ap()
            for n, a in arrays.items()]
    out = nc.dram_tensor("out", x.shape, F32, kind="ExternalOutput").ap()
    build(nc, *args, out)
    r = run_bass_kernel_spmd(nc, [{f"in_{n}": a for n, a in arrays.items()}], core_ids=[0])
    return r.results[0]["out"]
```

```python
from contextlib import ExitStack

import concourse.bass as bass
from concourse import mybir

F32 = mybir.dt.float32
F32R = mybir.dt.float32r
BF16 = mybir.dt.bfloat16
U8 = mybir.dt.uint8
I32 = mybir.dt.int32
ALU = mybir.AluOpType
ACT = mybir.ActivationFunctionType
AX_X = mybir.AxisListType.X

P = 128
STREAMS = 2
GB = 2
MASKED = 2.0 ** 100
LN_EPS = 1e-5

HI, LO = 0, 1
SPLIT_PRODUCTS = [(HI, HI), (HI, LO), (LO, HI)]


def build(nc, x, adj, attn_w, attn_bo, gcn_w, gcn_cols, gcn_tail, out):
    B, N, D = x.shape
    LAYERS = attn_w.shape[0]
    H, DH = 4, 64
    GH, DK = 8, 32
    DC = D // P
    NT = B // (GB * STREAMS)
    GF = GB * D
    THRESHOLD = 0.1
    GSCALE = float(DK) ** -0.5
    NORM2_MIN = 1e-16
    assert N == P and DC == 2 and H * DH == D and GH * DK == D
    WQ, WK, WV, WO = range(4)
    WM, WMQ, WMK, WG = range(4)
    RAW_MT, RAW_M, RAW_QT, RAW_KT = range(4)

    with ExitStack() as ctx:
        def sb(name, shape, dt=F32):
            return ctx.enter_context(nc.sbuf_tensor(name, shape, dt))

        def sem(name):
            return ctx.enter_context(nc.semaphore(name))

        def sems(name):
            return [sem(f"{name}{s}") for s in range(STREAMS)]

        w_part = [sb("w_hi", [P, 4, DC, D], F32R), sb("w_lo", [P, 4, DC, D], F32R)]
        raw_w = sb("raw_w", [P, 4, DC, D])
        raw_g = sb("raw_g", [P, DC, D])
        bias_rows = sb("bias_rows", [P, D])
        ident = sb("ident", [P, P])
        ident_bf = sb("ident_bf", [P, P], BF16)
        head_ones = sb("head_ones", [P, P])
        tail_w = sb("tail_w", [P, P])
        cols = sb("cols", [P, 4, DC])
        fused_b = sb("fused_b", [P, 2, DC])
        gb_wide = sb("gb_wide", [P, DC, P])
        eps_col = sb("eps_col", [P, 1])

        def per_stream(name, shape, dt=F32):
            return [sb(f"{name}{s}", shape, dt) for s in range(STREAMS)]

        stage = per_stream("stage", [P, GB, D])
        y_sum = per_stream("y_sum", [P, GF])
        x_keep = per_stream("x_keep", [P, GF])
        x_new = per_stream("x_new", [P, GF])
        xt = [[sb(f"xt_hi{s}", [P, DC, GB * N], F32R), sb(f"xt_lo{s}", [P, DC, GB * N], F32R)]
              for s in range(STREAMS)]
        ot = [[sb(f"ot_hi{s}", [P, DC, GB * N], F32R), sb(f"ot_lo{s}", [P, DC, GB * N], F32R)]
              for s in range(STREAMS)]
        qt = per_stream("qt", [P, DC, GB * N])
        kt = per_stream("kt", [P, DC, GB * N])
        v_rows = per_stream("v_rows", [P, GF])
        probs_all = sb("probs_all", [P, STREAMS, GB * H * N])
        probs_t_all = sb("probs_t_all", [P, STREAMS, GB * H * N])
        k_part = per_stream("k_part", [P, 2, DC, GB, N], F32R)
        n_part = per_stream("n_part", [P, 2, DC, GB, N], F32R)
        pair_diag = per_stream("pair_diag", [P, 2, 2, DC, GB, N], F32R)
        k_diag = per_stream("k_diag", [P, 4, 2, DC, GB, N], F32R)
        n_diag = per_stream("n_diag", [P, 4, 2, DC, GB, N], F32R)
        mask_words = per_stream("mask_words", [P, GB, N // 4], I32)
        mask_raw = [mask_words[s][:].bitcast(U8) for s in range(STREAMS)]
        mask_add = per_stream("mask_add", [P, GB, N], BF16)
        neg_max = per_stream("neg_max", [P, 8])
        row_sum = per_stream("row_sum", [P, GB, GH])
        gate_sum = per_stream("gate_sum", [P, GB, GH])
        out_t = per_stream("out_t", [P, DC, GB * N])
        rcp = per_stream("rcp", [P, GB * GH])
        total = per_stream("total", [P, GB * GH])
        keep = per_stream("keep", [P, GB, 1])
        bn = per_stream("bn", [P, GB, 6])
        mean_var = per_stream("mean_var", [P, GB, 2])
        log_var = per_stream("log_var", [P, GB])
        rstd = per_stream("rstd", [P, GB])

        probs = [probs_all[:, s].rearrange("p (b h j) -> p b h j", b=GB, h=H) for s in range(STREAMS)]
        probs_t = [probs_t_all[:, s].rearrange("p (b h i) -> p b h i", b=GB, h=H) for s in range(STREAMS)]
        flat = {name: [v[s][:].rearrange("p c n -> p (c n)") for s in range(STREAMS)]
                for name, v in (("m", qt), ("sq", kt))}

        psum = [ctx.enter_context(nc.psum_tensor(f"psum{s}", [P, 4, 512], F32)) for s in range(STREAMS)]
        SC0, SC1, WK0, WK1 = range(4)

        x_mid = nc.dram_tensor("x_mid", [B, N, D], F32, kind="Internal").ap()

        FREED, FULL = 1, 2
        loaded = sems("loaded")
        mask_loaded = sems("mask_loaded")
        kept = sems("kept")
        stored = sems("stored")
        const_ready = sem("const_ready")
        start_ready = sem("start_ready")
        raw_loaded = sem("raw_loaded")
        bias_loaded = sem("bias_loaded")
        w_hi_ready = sem("w_hi_ready")
        w_split = sem("w_split")
        wo_split = sem("wo_split")
        mask_ready = sems("mask_ready")
        x_keep_ready = sems("x_keep_ready")
        xt_psum = sems("xt_psum")
        xt_hi_ready, xt_lo_ready = sems("xt_hi_ready"), sems("xt_lo_ready")
        q_psum, k_psum, v_psum = sems("q_psum"), sems("k_psum"), sems("v_psum")
        v_ready = sems("v_ready")
        q_hi_ready, q_lo_ready = sems("q_hi_ready"), sems("q_lo_ready")
        k_hi_ready, k_lo_ready = sems("k_hi_ready"), sems("k_lo_ready")
        scores_psum = [sems(f"scores{b}_psum") for b in range(GB)]
        max_ready = [sems(f"max{b}_ready") for b in range(GB)]
        exp_ready = [sems(f"exp{b}_ready") for b in range(GB)]
        rcp_ready = [sems(f"rcp{b}_ready") for b in range(GB)]
        probs_ready = [sems(f"probs{b}_ready") for b in range(GB)]
        pt_psum = [sems(f"pt{b}_psum") for b in range(GB)]
        pt_ready = [sems(f"pt{b}_ready") for b in range(GB)]
        o_psum = sems("o_psum")
        ot_hi_ready, ot_lo_ready = sems("ot_hi_ready"), sems("ot_lo_ready")
        wo_psum = sems("wo_psum")
        y_ready = sems("y_ready")
        bn_ready, mv_ready = sems("bn_ready"), sems("mv_ready")
        log_ready, rstd_ready = sems("log_ready"), sems("rstd_ready")
        x_done = sems("x_done")
        graph_raw_loaded = sem("graph_raw_loaded")
        gb_wide_ready = sem("gb_wide_ready")
        fused_psum, fused_hi_ready, fused_ready = sem("fused_psum"), sem("fused_hi_ready"), sem("fused_ready")
        keep_ready = sems("keep_ready")
        m_psum, m_ready, sq_ready = sems("m_psum"), sems("m_ready"), sems("sq_ready")
        ss_psum, ss_ready, ss_log_ready = sems("ss_psum"), sems("ss_ready"), sems("ss_log_ready")
        inv_norm_ready, n_ready = sems("inv_norm_ready"), sems("n_ready")
        n_hi_ready, n_lo_ready = sems("n_hi_ready"), sems("n_lo_ready")
        k_spread, n_spread = sems("k_spread"), sems("n_spread")
        g_scores_psum = [sems(f"g_scores{b}_psum") for b in range(GB)]
        g_cos_psum = sems("g_cos_psum")
        gate_ready = [sems(f"gate{b}_ready") for b in range(GB)]
        gt_psum = [sems(f"gt{b}_psum") for b in range(GB)]
        gt_ready = [sems(f"gt{b}_ready") for b in range(GB)]
        g_out_psum = sems("g_out_psum")
        half_ready = sems("half_ready")
        out_t_ready = sems("out_t_ready")
        out_rows_psum = sems("out_rows_psum")
        scale_step = sems("scale_step")
        scaled_ready = sems("scaled_ready")

        ATTN_ITS = LAYERS * NT

        block = ctx.enter_context(nc.Block())

        def graphs(t, s):
            return bass.ds(t * (STREAMS * GB) + s * GB, GB)

        def credit(eng, *families):
            for family in families:
                for one in family:
                    eng.sem_inc(one, 1)

        @block.sync
        def _(sp):
            for s in range(STREAMS):
                sp.sem_inc(stored[s], 16)

            def load(t, it, s, source):
                sp.wait_ge(xt_psum[s], it + FREED)
                sp.wait_ge(x_keep_ready[s], it + FREED)
                if source is x_mid:
                    sp.wait_ge(stored[s], (it - NT) * 16 + 32)
                sp.dma_start(stage[s][:], source[graphs(t, s), :, :].rearrange("b n d -> n b d")) \
                  .then_inc(loaded[s], 16)
                sp.wait_ge(mask_ready[s], it + FREED)
                sp.dma_start(mask_words[s][:], adj[graphs(t, s), :, :].rearrange("b i j -> i b j")) \
                  .then_inc(mask_loaded[s], 16)

            def store(t, it, s, target):
                sp.wait_ge(x_done[s], it + FULL)
                sp.wait_ge(stored[s], it * 16 + 16)
                sp.dma_start(target[graphs(t, s), :, :].rearrange("b n d -> n b d"),
                             x_new[s][:].rearrange("p (b d) -> p b d", b=GB)).then_inc(stored[s], 16)

            def load_raw(layer):
                if not isinstance(layer, int) or layer > 0:
                    sp.wait_ge(wo_split, layer)
                sp.dma_start(raw_w[:], attn_w[bass.ds(layer, 1)].rearrange("l m (c p) o -> p (l m) c o", p=P)) \
                  .then_inc(raw_loaded, 16)

            def load_bias(layer):
                for s in range(STREAMS):
                    sp.wait_ge(x_keep_ready[s], layer * NT + FREED)
                sp.dma_start(bias_rows[:], attn_bo[bass.ds(layer, 1)].rearrange("l p o -> p (l o)")) \
                  .then_inc(bias_loaded, 16)

            def store_both(layer, t):
                for s in range(STREAMS):
                    store(t, layer * NT + t, s, x_mid)

            def sweep(layer, source, load_next_weights):
                base = layer * NT
                for s in range(STREAMS):
                    load(0, base, s, source)
                load_bias(layer)
                if source is x_mid:
                    store_both(layer - 1, NT - 2)
                for s in range(STREAMS):
                    load(1, base + 1, s, source)
                if source is x_mid:
                    store_both(layer - 1, NT - 1)
                load_next_weights()
                with sp.Fori(2, NT) as t:
                    for s in range(STREAMS):
                        load(t, base + t, s, source)
                        store(t - 2, base + t - 2, s, x_mid)

            def load_graph_weights():
                sp.wait_ge(wo_split, LAYERS)
                sp.dma_start(raw_w[:], gcn_w[0:4].rearrange("m (c p) o -> p m c o", p=P)).then_inc(graph_raw_loaded, 16)
                sp.dma_start(raw_g[:], gcn_w[4].rearrange("(c p) o -> p c o", p=P)).then_inc(graph_raw_loaded, 16)
                sp.dma_start(cols[:], gcn_cols).then_inc(graph_raw_loaded, 16)
                sp.wait_ge(const_ready, 9)
                for r in range(P // DK):
                    sp.dma_start(tail_w[r * DK:(r + 1) * DK, r * DK:(r + 1) * DK], gcn_tail) \
                      .then_inc(graph_raw_loaded, 16)

            load_raw(0)
            sweep(0, x, lambda: load_raw(1))
            with sp.Fori(1, LAYERS - 1) as layer:
                sweep(layer, x_mid, lambda: load_raw(layer + 1))
            sweep(LAYERS - 1, x_mid, load_graph_weights)

            def graph_load(t, s):
                sp.wait_ge(xt_psum[s], ATTN_ITS + t + FREED)
                sp.wait_ge(x_keep_ready[s], ATTN_ITS + FREED)
                sp.wait_ge(stored[s], (ATTN_ITS - NT + t) * 16 + 32)
                sp.dma_start(stage[s][:], x_mid[graphs(t, s), :, :].rearrange("b n d -> n b d")).then_inc(loaded[s], 16)
                sp.wait_ge(keep_ready[s], t + FREED)
                sp.wait_ge(mask_ready[s], ATTN_ITS + t + FREED)
                sp.dma_start(mask_words[s][:], adj[graphs(t, s), :, :].rearrange("b i j -> i b j")) \
                  .then_inc(mask_loaded[s], 16)

            def load_keep(t, s):
                sp.wait_ge(y_ready[s], ATTN_ITS + t + FREED)
                sp.dma_start(x_keep[s][:].rearrange("p (b d) -> p b d", b=GB),
                             x_mid[graphs(t, s), :, :].rearrange("b n d -> n b d")).then_inc(kept[s], 16)

            def spread(t, s, count, part, diag, hi_ready, lo_ready, used, done):
                sp.wait_ge(hi_ready[s], count + FULL)
                sp.wait_ge(lo_ready[s], count + FULL)
                sp.wait_ge(used[s], t * 2 + FREED)
                for r in range(4):
                    rows = slice(r * DK, (r + 1) * DK)
                    sp.dma_start(diag[s][rows, r].rearrange("p w c b j -> p (w c b j)").bitcast(F32),
                                 part[s][rows].rearrange("p w c b j -> p (w c b j)").bitcast(F32)).then_inc(done[s], 16)

            def graph_steps(t, s):
                spread(t, s, ATTN_ITS + t, k_part, k_diag, k_hi_ready, k_lo_ready, g_scores_psum[GB - 1], k_spread)
                spread(t, s, t, n_part, n_diag, n_hi_ready, n_lo_ready, g_cos_psum, n_spread)
                load_keep(t, s)

            sp.wait_ge(const_ready, 13)
            for s in range(STREAMS):
                graph_load(0, s)
            store_both(LAYERS - 1, NT - 2)
            store_both(LAYERS - 1, NT - 1)
            for s in range(STREAMS):
                graph_load(1, s)
                graph_steps(0, s)
            with sp.Fori(2, NT) as t:
                for s in range(STREAMS):
                    graph_load(t, s)
                    graph_steps(t - 1, s)
                    store(t - 2, ATTN_ITS + t - 2, s, out)
            for s in range(STREAMS):
                graph_steps(NT - 1, s)
                store(NT - 2, ATTN_ITS + NT - 2, s, out)
            for s in range(STREAMS):
                store(NT - 1, ATTN_ITS + NT - 1, s, out)
            for s in range(STREAMS):
                sp.wait_ge(stored[s], (ATTN_ITS + NT) * 16 + 16)

        @block.gpsimd
        def _(pool):
            credit(pool, mask_ready, x_keep_ready, keep_ready, x_done)
            pool.memset(ident[:], 0.0).then_inc(const_ready, 1)
            pool.wait_ge(const_ready, 1)
            pool.affine_select(out=ident[:], in_=ident[:], compare_op=ALU.not_equal, fill=1.0, base=0,
                               pattern=[[-1, P]], channel_multiplier=1).then_inc(const_ready, 1)
            pool.wait_ge(const_ready, 2)
            pool.tensor_copy(ident_bf[:], ident[:]).then_inc(const_ready, 1)
            pool.memset(tail_w[:], 0.0).then_inc(const_ready, 1)
            pool.memset(head_ones[:], 0.0).then_inc(const_ready, 1)
            pool.wait_ge(const_ready, 5)
            for r in range(P // DK):
                pool.memset(head_ones[r * DK:(r + 1) * DK, r * DK:(r + 1) * DK], 1.0).then_inc(const_ready, 1)
                pool.wait_ge(const_ready, 6 + r)
            for s in range(STREAMS):
                for diag in (k_diag, n_diag):
                    pool.memset(diag[s][:].rearrange("p r w c b j -> p (r w c b j)").bitcast(F32), 0.0) \
                        .then_inc(const_ready, 1)

            def mask_term(it, s):
                landed, freed = it * 16 + 16, it + FREED
                pool.compute_val(landed)
                pool.compute_val(freed)
                pool.wait_ge(const_ready, 9)
                pool.wait_ge(mask_loaded[s], landed)
                pool.wait_ge(scores_psum[GB - 1][s], freed)
                pool.tensor_scalar(mask_add[s][:], mask_raw[s], -1.0, MASKED, ALU.add, ALU.mult) \
                    .then_inc(mask_ready[s], 1)

            def add_bias(it, s, layer):
                pool.wait_ge(bias_loaded, layer * 16 + 16)
                pool.wait_ge(loaded[s], it * 16 + 16)
                pool.wait_ge(y_ready[s], it + FREED)
                pool.tensor_tensor(x_keep[s][:].rearrange("p (b f) -> p b f", b=GB), stage[s][:],
                                   bias_rows[:].unsqueeze(1).to_broadcast([P, GB, D]), ALU.add) \
                    .then_inc(x_keep_ready[s], 1)

            def norm_rows(it, s):
                full, unstored = it + FULL, it * 16 + 16
                pool.compute_val(full)
                pool.compute_val(unstored)
                pool.wait_ge(const_ready, 9)
                pool.wait_ge(rstd_ready[s], full)
                pool.wait_ge(stored[s], unstored)
                for b in range(GB):
                    last = pool.tensor_scalar(x_new[s][:, b * D:(b + 1) * D], y_sum[s][:, b * D:(b + 1) * D],
                                              mean_var[s][:, b, 0:1], rstd[s][:, b:b + 1], ALU.subtract, ALU.mult)
                last.then_inc(x_done[s], 1)

            def attention(before, now, nxt, next_layer):
                for s, other, summed in ((0, 1, before), (1, 0, now)):
                    if nxt is not None:
                        mask_term(nxt, s)
                    if summed is not None:
                        norm_rows(summed, other)
                    if nxt is not None:
                        add_bias(nxt, s, next_layer)

            attention(None, None, 0, 0)
            attention(None, 0, 1, 0)
            with pool.Fori(0, LAYERS - 1) as layer:
                first, after = layer * NT, layer * NT + NT
                with pool.Fori(1, NT - 1) as t:
                    attention(first + t - 1, first + t, first + t + 1, layer)
                attention(after - 2, after - 1, after, layer + 1)
                attention(after - 1, after, after + 1, layer + 1)
            first = (LAYERS - 1) * NT
            with pool.Fori(1, NT - 1) as t:
                attention(first + t - 1, first + t, first + t + 1, LAYERS - 1)
            attention(ATTN_ITS - 2, ATTN_ITS - 1, None, None)
            norm_rows(ATTN_ITS - 1, 1)

            def graph_masks(t, s):
                landed, summed, added = t * 16 + (ATTN_ITS * 16 + 16), t + (ATTN_ITS + FREED), t * 2 + FREED
                for count in (landed, summed, added):
                    pool.compute_val(count)
                pool.wait_ge(const_ready, 9)
                pool.wait_ge(mask_loaded[s], landed)
                pool.wait_ge(y_ready[s], summed)
                pool.tensor_scalar(keep[s][:], mask_raw[s][:, :, 0:1], -1.0, 1.0, ALU.mult, ALU.add) \
                    .then_inc(keep_ready[s], 1)
                pool.wait_ge(scores_psum[GB - 1][s], ATTN_ITS + FREED)
                pool.wait_ge(g_scores_psum[GB - 1][s], added)
                pool.tensor_scalar(mask_add[s][:], mask_raw[s], -MASKED, 0.0, ALU.mult, ALU.add) \
                    .then_inc(mask_ready[s], 1)

            def graph(now, nxt):
                for s in range(STREAMS):
                    if nxt is not None:
                        graph_masks(nxt, s)
                    if now is not None:
                        norm_rows(ATTN_ITS + now, s)

            graph(None, 0)
            with pool.Fori(0, NT - 1) as t:
                graph(t, t + 1)
            graph(NT - 1, None)

        @block.tensor
        def _(pe):
            credit(pe, xt_psum, v_psum, *scores_psum, *pt_psum, o_psum, wo_psum, *g_scores_psum, g_cos_psum, *gt_psum)
            credit(pe, q_psum, k_psum, m_psum, ss_psum, g_out_psum, out_rows_psum)

            def split_product(dst, left, right):
                n = len(SPLIT_PRODUCTS) * DC
                for i, (a, b) in enumerate(SPLIT_PRODUCTS):
                    for c in range(DC):
                        k = i * DC + c
                        last = pe.matmul(dst, left[a](c), right[b](c), start=(k == 0), stop=(k == n - 1))
                return last

            def transpose_rows(s, bank, rows):
                for b in range(GB):
                    for c in range(DC):
                        o = c * GB * N + b * N
                        last = pe.transpose(psum[s][:, bank, o:o + N], rows[:, b, c * P:(c + 1) * P], ident[:])
                return last

            def project_t(s, bank, slot):
                for m in range(DC):
                    last = split_product(
                        psum[s][:, bank, m * GB * N:(m + 1) * GB * N],
                        [lambda c, w=w: w[:, slot, c, m * P:(m + 1) * P] for w in w_part],
                        [lambda c, v=v: v[:, c, :] for v in xt[s]])
                return last

            def project_rows(s, bank, left, slot):
                for b in range(GB):
                    last = split_product(
                        psum[s][:, bank, b * D:(b + 1) * D],
                        [lambda c, v=v: v[:, c, b * N:(b + 1) * N] for v in left],
                        [lambda c, w=w: w[:, slot, c, :] for w in w_part])
                return last

            def transpose_x(it, s):
                pe.wait_ge(loaded[s], it * 16 + 16)
                transpose_rows(s, SC1, stage[s]).then_inc(xt_psum[s], 1)

            def project_qk(it, s, layer):
                pe.wait_ge(w_split, layer + 1)
                pe.wait_ge(xt_hi_ready[s], it + FULL)
                pe.wait_ge(xt_lo_ready[s], it + FULL)
                project_t(s, WK1, WQ).then_inc(q_psum[s], 1)
                project_t(s, WK0, WK).then_inc(k_psum[s], 1)

            def project_v(it, s):
                pe.wait_ge(ot_hi_ready[s], it + FREED)
                pe.wait_ge(ot_lo_ready[s], it + FREED)
                project_rows(s, SC0, xt[s], WV).then_inc(v_psum[s], 1)

            def scores(it, s):
                pe.wait_ge(mask_ready[s], it + FULL)
                pe.wait_ge(q_hi_ready[s], it + FULL)
                pe.wait_ge(q_lo_ready[s], it + FULL)
                pe.wait_ge(k_hi_ready[s], it + FULL)
                pe.wait_ge(k_lo_ready[s], it + FULL)
                for b in range(GB):
                    if b == 0:
                        pe.wait_ge(v_ready[s], it + FULL)
                    else:
                        pe.wait_ge(y_ready[s], it + FREED)
                    pe.matmul(psum[s][:, SC0 + b, :].rearrange("p (h j) -> p h j", h=H), ident_bf[:],
                              mask_add[s][:, b, :].unsqueeze(1).to_broadcast([P, H, N]), start=True, stop=True)
                    for left, right in SPLIT_PRODUCTS:
                        for c in range(DC):
                            last = pe.matmul(psum[s][:, SC0 + b, c * 2 * N:(c + 1) * 2 * N]
                                             .rearrange("p (r j) -> p r j", r=2),
                                             k_part[s][:, left, c, b], pair_diag[s][:, :, right, c, b],
                                             start=False, stop=True, skip_group_check=True)
                    last.then_inc(scores_psum[b][s], 1)

            def transpose_probs(it, s):
                for b in range(GB):
                    pe.wait_ge(probs_ready[b][s], it + FULL)
                    for h in range(H):
                        last = pe.transpose(psum[s][:, WK0 + b, h * N:(h + 1) * N], probs[s][:, b, h, :], ident[:])
                    last.then_inc(pt_psum[b][s], 1)

            def weighted_values(it, s):
                for b in range(GB):
                    pe.wait_ge(pt_ready[b][s], it + FULL)
                    for h in range(H):
                        c, r = divmod(h, 2)
                        o = c * GB * N + b * N
                        last = pe.matmul(psum[s][r * DH:(r + 1) * DH, SC0, o:o + N],
                                         v_rows[s][:, b * D + h * DH:b * D + (h + 1) * DH], probs_t[s][:, b, h, :],
                                         start=True, stop=True)
                last.then_inc(o_psum[s], 1)

            def project_out(it, s, layer):
                pe.wait_ge(wo_split, layer + 1)
                pe.wait_ge(ot_hi_ready[s], it + FULL)
                pe.wait_ge(ot_lo_ready[s], it + FULL)
                project_rows(s, SC1, ot[s], WO).then_inc(wo_psum[s], 1)

            def attention(now, nxt, layer, next_layer):
                for s, other, ending in ((0, 1, now), (1, 0, nxt)):
                    if nxt is not None:
                        transpose_x(nxt, s)
                    if ending is not None:
                        scores(ending, other)
                    if now is not None:
                        weighted_values(now, s)
                    if nxt is not None:
                        project_qk(nxt, s, next_layer)
                    if now is not None:
                        project_out(now, s, layer)
                    if nxt is not None:
                        project_v(nxt, s)
                    if ending is not None:
                        transpose_probs(ending, other)

            def fuse_weights():
                bank = psum[0]
                pe.wait_ge(graph_raw_loaded, 16 * 7)
                pe.wait_ge(gb_wide_ready, 1)
                for i in range(2):
                    for m in range(DC):
                        for c in range(DC):
                            pe.matmul(bank[:, i, m * D:(m + 1) * D], raw_w[:, RAW_M, c, m * P:(m + 1) * P],
                                      raw_w[:, RAW_QT + i, c, :], start=(c == 0), stop=(c == DC - 1))
                for m in range(DC):
                    for c in range(DC):
                        o = m * D + c * P
                        pe.matmul(bank[:, 2, o:o + P], raw_g[:, c, m * P:(m + 1) * P], tail_w[:], start=True, stop=True)
                for i in range(2):
                    for m in range(DC):
                        for c in range(DC):
                            pe.matmul(bank[:, 3, i * DC + m:i * DC + m + 1], raw_w[:, RAW_QT + i, c, m * P:(m + 1) * P],
                                      cols[:, 0, c:c + 1], start=(c == 0), stop=(c == DC - 1))
                for c in range(DC):
                    last = pe.matmul(bank[:, 3, P + c * P:P + (c + 1) * P], gb_wide[:, c, :], tail_w[:],
                                     start=True, stop=True)
                last.then_inc(fused_psum, 1)

            def graph_transpose_x(t, s):
                pe.wait_ge(loaded[s], (ATTN_ITS + t) * 16 + 16)
                transpose_rows(s, 3, stage[s]).then_inc(xt_psum[s], 1)

            def graph_project_m(t, s):
                pe.wait_ge(xt_hi_ready[s], ATTN_ITS + t + FULL)
                pe.wait_ge(xt_lo_ready[s], ATTN_ITS + t + FULL)
                project_t(s, 3, WM).then_inc(m_psum[s], 1)

            def graph_project_q(t, s):
                project_t(s, 0, WMQ).then_inc(q_psum[s], 1)

            def graph_project_k(t, s):
                project_t(s, 1, WMK).then_inc(k_psum[s], 1)

            def square_sums(t, s):
                pe.wait_ge(scaled_ready[s], t + FREED)
                pe.wait_ge(sq_ready[s], t + FULL)
                for c in range(DC):
                    last = pe.matmul(psum[s][:, 2, c * GB * N:(c + 1) * GB * N], head_ones[:], kt[s][:, c, :],
                                     start=True, stop=True)
                last.then_inc(ss_psum[s], 1)

            def graph_values(t, s):
                pe.wait_ge(m_ready[s], t + FULL)
                project_rows(s, 3, xt[s], WG).then_inc(v_psum[s], 1)

            def graph_scores(t, s, half):
                if half == 0:
                    pe.wait_ge(mask_ready[s], ATTN_ITS + t + FULL)
                    pe.wait_ge(q_hi_ready[s], ATTN_ITS + t + FULL)
                    pe.wait_ge(q_lo_ready[s], ATTN_ITS + t + FULL)
                    pe.wait_ge(k_spread[s], t * 64 + 64)
                for b in range(GB):
                    pe.matmul(psum[s][:, b, :].rearrange("p (r j) -> p r j", r=4), ident_bf[:],
                              mask_add[s][:, b, :].unsqueeze(1).to_broadcast([P, 4, N]), start=True, stop=True)
                    for left, right in SPLIT_PRODUCTS:
                        last = pe.matmul(psum[s][:, b, :].rearrange("p (r j) -> p r j", r=4), ot[s][left][:, half, b * N:(b + 1) * N],
                                         k_diag[s][:, :, right, half, b],
                                         start=False, stop=True, skip_group_check=True)
                    last.then_inc(g_scores_psum[b][s], 1)

            def graph_cosines(t, s, half):
                if half == 0:
                    pe.wait_ge(n_spread[s], t * 64 + 64)
                    order = ((0, None), (1, v_ready[s]))
                    free_count = ATTN_ITS + t + FULL
                else:
                    order = ((1, None), (0, half_ready[s]))
                    free_count = t + FULL
                for b, bank_free in order:
                    if bank_free is not None:
                        pe.wait_ge(bank_free, free_count)
                    for i, (left, right) in enumerate(SPLIT_PRODUCTS):
                        last = pe.matmul(psum[s][:, 2 + b, :].rearrange("p (r j) -> p r j", r=4), n_part[s][:, left, half, b],
                                         n_diag[s][:, :, right, half, b],
                                         start=(i == 0), stop=(i == len(SPLIT_PRODUCTS) - 1))
                last.then_inc(g_cos_psum[s], 1)

            def transpose_gates(t, s, half):
                for b in range(GB):
                    pe.wait_ge(gate_ready[b][s], t * 2 + half + FULL)
                    for r in range(4):
                        last = pe.transpose(psum[s][:, b, r * N:(r + 1) * N], probs[s][:, b, r, :], ident[:])
                    last.then_inc(gt_psum[b][s], 1)

            def gated_values(t, s, half):
                for b in range(GB):
                    pe.wait_ge(gt_ready[b][s], t * 2 + half + FULL)
                    for r in range(4):
                        v = b * D + (4 * half + r) * DK
                        o = (half * GB + b) * N
                        last = pe.matmul(psum[s][r * DK:(r + 1) * DK, 2, o:o + N], v_rows[s][:, v:v + DK],
                                         probs_t[s][:, b, r, :], start=True, stop=True)
                last.then_inc(g_out_psum[s], 1)

            def transpose_out(t, s):
                pe.wait_ge(half_ready[s], t + FULL)
                pe.wait_ge(out_t_ready[s], t + FULL)
                for b in range(GB):
                    for c in range(DC):
                        o = b * D + c * P
                        last = pe.transpose(psum[s][:, 2, o:o + P], out_t[s][:, c, b * N:(b + 1) * N], ident[:])
                last.then_inc(out_rows_psum[s], 1)

            def graph(now, nxt):
                for s, other, ending in ((0, 1, now), (1, 0, nxt)):
                    if nxt is not None:
                        graph_transpose_x(nxt, s)
                    if now is not None:
                        gated_values(now, s, 1)
                    if nxt is not None:
                        graph_project_m(nxt, s)
                    if now is not None:
                        transpose_out(now, s)
                    if nxt is not None:
                        graph_project_k(nxt, s)
                        square_sums(nxt, s)
                        graph_project_q(nxt, s)
                    if ending is not None:
                        transpose_gates(ending, other, 0)
                    if nxt is not None:
                        graph_values(nxt, s)
                    if ending is not None:
                        gated_values(ending, other, 0)
                        graph_scores(ending, other, 1)
                        graph_cosines(ending, other, 1)
                    if nxt is not None:
                        graph_scores(nxt, s, 0)
                        graph_cosines(nxt, s, 0)
                    if ending is not None:
                        transpose_gates(ending, other, 1)

            pe.wait_ge(const_ready, 9)
            attention(None, 0, 0, 0)
            attention(0, 1, 0, 0)
            with pe.Fori(0, LAYERS - 1) as layer:
                first, after = layer * NT, layer * NT + NT
                with pe.Fori(1, NT - 1) as t:
                    attention(first + t, first + t + 1, layer, layer)
                attention(after - 1, after, layer, layer + 1)
                attention(after, after + 1, layer + 1, layer + 1)
            first = (LAYERS - 1) * NT
            with pe.Fori(1, NT - 1) as t:
                attention(first + t, first + t + 1, LAYERS - 1, LAYERS - 1)
            attention(ATTN_ITS - 1, None, LAYERS - 1, None)

            for s in range(STREAMS):
                pe.wait_ge(y_ready[s], ATTN_ITS + FREED)
            fuse_weights()
            pe.wait_ge(fused_ready, 1)
            graph(None, 0)
            with pe.Fori(0, NT - 1) as t:
                graph(t, t + 1)
            graph(NT - 1, None)

        @block.scalar
        def _(act):
            credit(act, xt_hi_ready, v_ready, *exp_ready, pt_ready[1], ot_hi_ready, log_ready, rstd_ready,
                   m_ready, sq_ready, ss_log_ready, inv_norm_ready, out_t_ready, q_hi_ready, k_hi_ready, n_hi_ready,
                   gt_ready[1])

            def split_hi(it, s, bank):
                act.wait_ge(xt_psum[s], it + FULL)
                act.wait_ge(v_psum[s], it + FREED)
                act.activation(xt[s][HI][:].rearrange("p c n -> p (c n)"), psum[s][:, bank, :], ACT.Copy) \
                   .then_inc(xt_hi_ready[s], 1)

            def q_hi(it, s):
                act.wait_ge(q_psum[s], it + FULL)
                act.activation(k_part[s][:, HI].rearrange("p c b n -> p (c b n)"), psum[s][:, WK1, :], ACT.Copy,
                               scale=float(DH) ** -0.5).then_inc(q_hi_ready[s], 1)

            def k_hi(it, s):
                act.wait_ge(k_psum[s], it + FULL)
                for r in range(2):
                    rows = slice(r * DH, (r + 1) * DH)
                    last = act.activation(pair_diag[s][rows, r, HI].rearrange("p c b n -> p (c b n)"),
                                          psum[s][rows, WK0, :], ACT.Copy)
                last.then_inc(k_hi_ready[s], 1)

            def v_out(it, s):
                act.wait_ge(v_psum[s], it + FULL)
                act.wait_ge(o_psum[s], it + FREED)
                act.activation(v_rows[s][:], psum[s][:, SC0, :], ACT.Copy).then_inc(v_ready[s], 1)

            def exps(it, s, b):
                act.wait_ge(max_ready[b][s], it + FULL)
                act.wait_ge(pt_psum[b][s], it + FREED)
                for h in range(H):
                    last = act.activation(probs[s][:, b, h, :], psum[s][:, SC0 + b, h * N:(h + 1) * N], ACT.Exp,
                                          bias=neg_max[s][:, b * H + h:b * H + h + 1],
                                          accum_out=row_sum[s][:, b, h:h + 1])
                last.then_inc(exp_ready[b][s], 1)

            def pt1(it, s):
                act.wait_ge(pt_psum[1][s], it + FULL)
                act.activation(probs_t[s][:, 1].rearrange("p h i -> p (h i)"), psum[s][:, WK1, :], ACT.Copy) \
                   .then_inc(pt_ready[1][s], 1)

            def ot_hi(it, s):
                act.wait_ge(o_psum[s], it + FULL)
                act.wait_ge(wo_psum[s], it + FREED)
                act.activation(ot[s][HI][:].rearrange("p c n -> p (c n)"), psum[s][:, SC0, :], ACT.Copy) \
                   .then_inc(ot_hi_ready[s], 1)

            def rstd_of(it, s):
                act.wait_ge(mv_ready[s], it + FULL)
                act.activation(log_var[s][:], mean_var[s][:, :, 1], ACT.Ln, bias=eps_col[:, 0:1]) \
                   .then_inc(log_ready[s], 1)
                act.wait_ge(log_ready[s], it + FULL)
                act.activation(rstd[s][:], log_var[s][:], ACT.Exp, scale=-0.5).then_inc(rstd_ready[s], 1)

            def attention(before, now, nxt):
                for s, other, ending, summed in ((0, 1, now, before), (1, 0, nxt, now)):
                    if now is not None:
                        pt1(now, s)
                    if nxt is not None:
                        split_hi(nxt, s, SC1)
                    if ending is not None:
                        exps(ending, other, 0)
                    if now is not None:
                        ot_hi(now, s)
                    if ending is not None:
                        exps(ending, other, 1)
                    if nxt is not None:
                        q_hi(nxt, s)
                        k_hi(nxt, s)
                    if summed is not None:
                        rstd_of(summed, other)
                    if nxt is not None:
                        v_out(nxt, s)

            def m_out(t, s):
                act.wait_ge(m_psum[s], t + FULL)
                act.wait_ge(n_lo_ready[s], t + FREED)
                for c in range(DC):
                    last = act.activation(qt[s][:, c, :], psum[s][:, 3, c * GB * N:(c + 1) * GB * N], ACT.Identity,
                                          bias=cols[:, 0, c:c + 1])
                last.then_inc(m_ready[s], 1)
                act.wait_ge(m_ready[s], t + FULL)
                act.wait_ge(n_ready[s], t + FREED)
                act.activation(flat["sq"][s], flat["m"][s], ACT.Square).then_inc(sq_ready[s], 1)

            def graph_q_hi(t, s):
                act.wait_ge(q_psum[s], ATTN_ITS + t + FULL)
                act.wait_ge(g_scores_psum[GB - 1][s], t * 2 + FREED)
                for c in range(DC):
                    last = act.activation(ot[s][HI][:, c, :], psum[s][:, 0, c * GB * N:(c + 1) * GB * N], ACT.Identity,
                                          bias=fused_b[:, 0, c:c + 1])
                last.then_inc(q_hi_ready[s], 1)

            def graph_k_hi(t, s):
                act.wait_ge(k_psum[s], ATTN_ITS + t + FULL)
                act.wait_ge(g_scores_psum[GB - 1][s], t * 2 + FREED)
                for c in range(DC):
                    last = act.activation(k_part[s][:, HI, c].rearrange("p b n -> p (b n)"),
                                          psum[s][:, 1, c * GB * N:(c + 1) * GB * N], ACT.Identity,
                                          bias=fused_b[:, 1, c:c + 1])
                last.then_inc(k_hi_ready[s], 1)

            def inverse_norms(t, s):
                act.wait_ge(ss_ready[s], t + FULL)
                act.activation(flat["sq"][s], flat["sq"][s], ACT.Ln).then_inc(ss_log_ready[s], 1)
                act.wait_ge(ss_log_ready[s], t + FULL)
                act.activation(flat["sq"][s], flat["sq"][s], ACT.Exp, scale=-0.5).then_inc(inv_norm_ready[s], 1)

            def n_hi(t, s):
                act.wait_ge(n_ready[s], t + FULL)
                act.wait_ge(g_cos_psum[s], t * 2 + FREED)
                act.activation(n_part[s][:, HI].rearrange("p c b n -> p (c b n)"), flat["m"][s], ACT.Copy) \
                   .then_inc(n_hi_ready[s], 1)

            def graph_exps(t, s, half, b):
                act.wait_ge(max_ready[b][s], ATTN_ITS + t * 2 + half + FULL)
                if half == 0:
                    act.wait_ge(y_ready[s], ATTN_ITS + t + FREED)
                else:
                    act.wait_ge(gt_psum[b][s], t * 2 + half + FREED)
                for r in range(4):
                    h = 4 * half + r
                    last = act.activation(probs[s][:, b, r, :], psum[s][:, b, r * N:(r + 1) * N], ACT.Exp,
                                          bias=neg_max[s][:, b * 4 + r:b * 4 + r + 1],
                                          accum_out=row_sum[s][:, b, h:h + 1])
                last.then_inc(exp_ready[b][s], 1)

            def gt1(t, s, half):
                act.wait_ge(gt_psum[1][s], t * 2 + half + FULL)
                act.activation(probs_t[s][:, 1].rearrange("p r i -> p (r i)"), psum[s][:, 1, :], ACT.Copy) \
                   .then_inc(gt_ready[1][s], 1)

            def second_half(t, s):
                act.wait_ge(g_out_psum[s], t * 2 + 1 + FULL)
                act.wait_ge(out_rows_psum[s], t + FREED)
                act.activation(out_t[s][:, 1, :], psum[s][:, 2, GB * N:2 * GB * N], ACT.Copy) \
                   .then_inc(out_t_ready[s], 1)

            def graph(now, nxt):
                for s, other, ending in ((0, 1, now), (1, 0, nxt)):
                    if ending is not None:
                        graph_exps(ending, other, 0, 0)
                    if nxt is not None:
                        split_hi(ATTN_ITS + nxt, s, 3)
                    if now is not None:
                        gt1(now, s, 1)
                    if ending is not None:
                        graph_exps(ending, other, 0, 1)
                    if now is not None:
                        second_half(now, s)
                    if nxt is not None:
                        m_out(nxt, s)
                        graph_k_hi(nxt, s)
                        inverse_norms(nxt, s)
                    if ending is not None:
                        gt1(ending, other, 0)
                    if nxt is not None:
                        n_hi(nxt, s)
                        graph_q_hi(nxt, s)
                    if ending is not None:
                        graph_exps(ending, other, 1, 0)
                        graph_exps(ending, other, 1, 1)
                    if now is not None:
                        rstd_of(ATTN_ITS + now, s)

            act.preload_act_table_set("natural_log_exp_and_others")
            act.wait_ge(start_ready, 3)
            attention(None, None, 0)
            attention(None, 0, 1)
            with act.Fori(0, LAYERS - 1) as layer:
                first, after = layer * NT, layer * NT + NT
                with act.Fori(1, NT - 1) as t:
                    attention(first + t - 1, first + t, first + t + 1)
                attention(after - 2, after - 1, after)
                attention(after - 1, after, after + 1)
            first = (LAYERS - 1) * NT
            with act.Fori(1, NT - 1) as t:
                attention(first + t - 1, first + t, first + t + 1)
            attention(ATTN_ITS - 2, ATTN_ITS - 1, None)
            rstd_of(ATTN_ITS - 1, 1)

            act.wait_ge(graph_raw_loaded, 16 * 7)
            graph(None, 0)
            with act.Fori(0, NT - 1) as t:
                graph(t, t + 1)
            graph(NT - 1, None)

        @block.vector
        def _(dve):
            credit(dve, xt_lo_ready, *max_ready, *rcp_ready, *probs_ready, pt_ready[0], ot_lo_ready, y_ready, bn_ready,
                   mv_ready, ss_ready, n_ready, q_lo_ready, k_lo_ready, n_lo_ready, *gate_ready, gt_ready[0], half_ready, scale_step, scaled_ready)

            def split_lo(it, s, bank):
                dve.wait_ge(xt_hi_ready[s], it + FULL)
                dve.tensor_tensor(xt[s][LO][:].rearrange("p c n -> p (c n)"), psum[s][:, bank, :],
                                  xt[s][HI][:].rearrange("p c n -> p (c n)").bitcast(F32), ALU.subtract) \
                   .then_inc(xt_lo_ready[s], 1)

            def q_lo(it, s):
                dve.wait_ge(q_hi_ready[s], it + FULL)
                dve.scalar_tensor_tensor(k_part[s][:, LO].rearrange("p c b n -> p (c b n)"), psum[s][:, WK1, :],
                                         float(DH) ** -0.5, k_part[s][:, HI].rearrange("p c b n -> p (c b n)")
                                         .bitcast(F32), ALU.mult, ALU.subtract).then_inc(q_lo_ready[s], 1)

            def k_lo(it, s):
                dve.wait_ge(k_hi_ready[s], it + FULL)
                for r in range(2):
                    rows = slice(r * DH, (r + 1) * DH)
                    last = dve.tensor_tensor(pair_diag[s][rows, r, LO].rearrange("p c b n -> p (c b n)"),
                                             psum[s][rows, WK0, :],
                                             pair_diag[s][rows, r, HI].rearrange("p c b n -> p (c b n)").bitcast(F32),
                                             ALU.subtract)
                last.then_inc(k_lo_ready[s], 1)

            def maxima(it, s, b):
                dve.wait_ge(scores_psum[b][s], it + FULL)
                dve.wait_ge(exp_ready[b][s], it + FREED)
                dve.tensor_reduce(neg_max[s][:, b * H:(b + 1) * H],
                                  psum[s][:, SC0 + b, :].rearrange("p (h j) -> p h j", h=H),
                                  AX_X, ALU.max, negate=True).then_inc(max_ready[b][s], 1)

            def normalise(it, s, b):
                r = rcp[s][:, b * H:(b + 1) * H]
                dve.wait_ge(exp_ready[b][s], it + FULL)
                dve.reciprocal(r, row_sum[s][:, b, 0:H]).then_inc(rcp_ready[b][s], 1)
                dve.wait_ge(rcp_ready[b][s], it + FULL)
                dve.tensor_tensor(probs[s][:, b], probs[s][:, b], r.unsqueeze(2).to_broadcast([P, H, N]), ALU.mult) \
                   .then_inc(probs_ready[b][s], 1)

            def pt0(it, s):
                dve.wait_ge(pt_psum[0][s], it + FULL)
                dve.tensor_copy(probs_t[s][:, 0].rearrange("p h i -> p (h i)"), psum[s][:, WK0, :]) \
                   .then_inc(pt_ready[0][s], 1)

            def ot_lo(it, s):
                dve.wait_ge(ot_hi_ready[s], it + FULL)
                dve.tensor_tensor(ot[s][LO][:].rearrange("p c n -> p (c n)"), psum[s][:, SC0, :],
                                  ot[s][HI][:].rearrange("p c n -> p (c n)").bitcast(F32), ALU.subtract) \
                   .then_inc(ot_lo_ready[s], 1)

            def residual(it, s):
                dve.wait_ge(wo_psum[s], it + FULL)
                dve.wait_ge(x_keep_ready[s], it + FULL)
                dve.wait_ge(x_done[s], it + FREED)
                dve.tensor_tensor(y_sum[s][:], psum[s][:, SC1, :], x_keep[s][:], ALU.add).then_inc(y_ready[s], 1)

            def statistics(it, s):
                dve.wait_ge(y_ready[s], it + FULL)
                for b in range(GB):
                    last = dve.bn_stats(bn[s][:, b, :], y_sum[s][:, b * D:(b + 1) * D])
                last.then_inc(bn_ready[s], 1)
                dve.wait_ge(start_ready, 3)
                dve.wait_ge(bn_ready[s], it + FULL)
                for b in range(GB):
                    last = dve.bn_aggr(mean_var[s][:, b, :], bn[s][:, b, :])
                last.then_inc(mv_ready[s], 1)

            def attention(before, now, nxt):
                for s, other, ending, summed in ((0, 1, now, before), (1, 0, nxt, now)):
                    if now is not None:
                        pt0(now, s)
                    if nxt is not None:
                        split_lo(nxt, s, SC1)
                    if ending is not None:
                        maxima(ending, other, 0)
                        maxima(ending, other, 1)
                    if summed is not None:
                        statistics(summed, other)
                    if ending is not None:
                        normalise(ending, other, 0)
                    if now is not None:
                        ot_lo(now, s)
                    if ending is not None:
                        normalise(ending, other, 1)
                    if nxt is not None:
                        q_lo(nxt, s)
                        k_lo(nxt, s)
                    if now is not None:
                        residual(now, s)

            def split_weights(slots, count, done):
                hi = w_part[HI][:, slots].rearrange("p m c o -> p (m c o)")
                lo = w_part[LO][:, slots].rearrange("p m c o -> p (m c o)")
                raw = raw_w[:, slots].rearrange("p m c o -> p (m c o)")
                dve.tensor_copy(hi, raw).then_inc(w_hi_ready, 1)
                dve.wait_ge(w_hi_ready, count)
                dve.tensor_tensor(lo, raw, hi.bitcast(F32), ALU.subtract).then_inc(done, 1)

            def split_qkv(layer):
                dve.wait_ge(raw_loaded, layer * 16 + 16)
                for s in range(STREAMS):
                    dve.wait_ge(v_psum[s], layer * NT + FREED)
                split_weights(slice(WQ, WO), layer * 2 + 1, w_split)

            def split_out(layer):
                for s in range(STREAMS):
                    dve.wait_ge(wo_psum[s], layer * NT + FREED)
                split_weights(slice(WO, WO + 1), layer * 2 + 2, wo_split)

            def split_fused():
                bank = psum[0]
                dve.wait_ge(fused_psum, 1)
                flat_w = [w[:].rearrange("p m c o -> p m (c o)") for w in w_part]
                dve.tensor_copy(flat_w[HI][:, WM, :], raw_w[:, RAW_MT].rearrange("p c o -> p (c o)"))
                dve.tensor_scalar(flat_w[HI][:, WMQ, :], bank[:, 0, :], GSCALE, None, ALU.mult)
                dve.tensor_copy(flat_w[HI][:, WMK:WG + 1, :], bank[:, 1:3, :]).then_inc(fused_hi_ready, 1)
                for c in range(DC):
                    dve.tensor_scalar(fused_b[:, 0, c:c + 1], bank[:, 3, c:c + 1], cols[:, 1, c:c + 1], GSCALE,
                                      ALU.add, ALU.mult)
                dve.tensor_tensor(fused_b[:, 1, :], bank[:, 3, DC:2 * DC], cols[:, 2, :], ALU.add)
                dve.tensor_copy(bias_rows[:], bank[:, 3, P:P + D])
                dve.wait_ge(fused_hi_ready, 1)
                dve.tensor_tensor(flat_w[LO][:, WM, :], raw_w[:, RAW_MT].rearrange("p c o -> p (c o)"),
                                  flat_w[HI][:, WM, :].bitcast(F32), ALU.subtract)
                dve.scalar_tensor_tensor(flat_w[LO][:, WMQ, :], bank[:, 0, :], GSCALE,
                                         flat_w[HI][:, WMQ, :].bitcast(F32), ALU.mult, ALU.subtract)
                dve.tensor_tensor(flat_w[LO][:, WMK:WG + 1, :], bank[:, 1:3, :],
                                  flat_w[HI][:, WMK:WG + 1, :].bitcast(F32), ALU.subtract).then_inc(fused_ready, 1)
                dve.wait_ge(fused_ready, 1)

            def graph_q_lo(t, s):
                dve.wait_ge(q_hi_ready[s], ATTN_ITS + t + FULL)
                for c in range(DC):
                    last = dve.scalar_tensor_tensor(ot[s][LO][:, c, :], psum[s][:, 0, c * GB * N:(c + 1) * GB * N],
                                                    fused_b[:, 0, c:c + 1], ot[s][HI][:, c, :].bitcast(F32),
                                                    ALU.add, ALU.subtract)
                last.then_inc(q_lo_ready[s], 1)

            def graph_k_lo(t, s):
                dve.wait_ge(k_hi_ready[s], ATTN_ITS + t + FULL)
                for c in range(DC):
                    last = dve.scalar_tensor_tensor(k_part[s][:, LO, c].rearrange("p b n -> p (b n)"),
                                                    psum[s][:, 1, c * GB * N:(c + 1) * GB * N], fused_b[:, 1, c:c + 1],
                                                    k_part[s][:, HI, c].rearrange("p b n -> p (b n)").bitcast(F32),
                                                    ALU.add, ALU.subtract)
                last.then_inc(k_lo_ready[s], 1)

            def norm_guard(t, s):
                dve.wait_ge(ss_psum[s], t + FULL)
                dve.tensor_scalar(flat["sq"][s], psum[s][:, 2, :], NORM2_MIN, None, ALU.max).then_inc(ss_ready[s], 1)

            def normalised(t, s):
                dve.wait_ge(inv_norm_ready[s], t + FULL)
                dve.tensor_tensor(flat["m"][s], flat["m"][s], flat["sq"][s], ALU.mult).then_inc(n_ready[s], 1)

            def n_lo(t, s):
                dve.wait_ge(n_hi_ready[s], t + FULL)
                dve.tensor_tensor(n_part[s][:, LO].rearrange("p c b n -> p (c b n)"), flat["m"][s],
                                  n_part[s][:, HI].rearrange("p c b n -> p (c b n)").bitcast(F32), ALU.subtract) \
                   .then_inc(n_lo_ready[s], 1)

            def graph_v(t, s):
                dve.wait_ge(v_psum[s], ATTN_ITS + t + FULL)
                dve.wait_ge(g_out_psum[s], t * 2 + FREED)
                dve.tensor_tensor(v_rows[s][:].rearrange("p (b f) -> p b f", b=GB),
                                  psum[s][:, 3, :].rearrange("p (b f) -> p b f", b=GB),
                                  bias_rows[:].unsqueeze(1).to_broadcast([P, GB, D]), ALU.add).then_inc(v_ready[s], 1)

            def graph_maxima(t, s, half, b):
                dve.wait_ge(g_scores_psum[b][s], t * 2 + half + FULL)
                dve.wait_ge(exp_ready[b][s], ATTN_ITS + t * 2 + half + FREED)
                dve.tensor_reduce(neg_max[s][:, b * 4:(b + 1) * 4], psum[s][:, b, :].rearrange("p (r j) -> p r j", r=4),
                                  AX_X, ALU.max, negate=True).then_inc(max_ready[b][s], 1)

            def gate(t, s, half, b):
                dve.wait_ge(exp_ready[b][s], ATTN_ITS + t * 2 + half + FULL)
                dve.wait_ge(g_cos_psum[s], t * 2 + half + FULL)
                for r in range(4):
                    h = 4 * half + r
                    last = dve.scalar_tensor_tensor(probs[s][:, b, r, :], psum[s][:, 2 + b, r * N:(r + 1) * N], THRESHOLD,
                                                    probs[s][:, b, r, :], ALU.is_gt, ALU.mult,
                                                    accum_out=gate_sum[s][:, b, h:h + 1])
                last.then_inc(gate_ready[b][s], 1)

            def gt0(t, s, half):
                dve.wait_ge(gt_psum[0][s], t * 2 + half + FULL)
                dve.tensor_copy(probs_t[s][:, 0].rearrange("p r i -> p (r i)"), psum[s][:, 0, :]) \
                   .then_inc(gt_ready[0][s], 1)

            def first_half(t, s):
                dve.wait_ge(g_out_psum[s], t * 2 + FULL)
                dve.wait_ge(out_rows_psum[s], t + FREED)
                dve.tensor_copy(out_t[s][:, 0, :], psum[s][:, 2, 0:GB * N]).then_inc(half_ready[s], 1)

            def output_scale(t, s):
                for b in range(GB):
                    dve.wait_ge(gate_ready[b][s], t * 2 + 1 + FULL)
                dve.tensor_tensor(total[s][:], gate_sum[s][:].rearrange("p b h -> p (b h)"),
                                  row_sum[s][:].rearrange("p b h -> p (b h)"), ALU.add).then_inc(scale_step[s], 1)
                dve.wait_ge(scale_step[s], t * 3 + FULL)
                dve.reciprocal(rcp[s][:], total[s][:]).then_inc(scale_step[s], 1)
                dve.wait_ge(scale_step[s], t * 3 + 1 + FULL)
                dve.wait_ge(keep_ready[s], t + FULL)
                dve.tensor_tensor(total[s][:].rearrange("p (b h) -> p b h", b=GB),
                                  rcp[s][:].rearrange("p (b h) -> p b h", b=GB),
                                  keep[s][:].to_broadcast([P, GB, GH]), ALU.mult).then_inc(scale_step[s], 1)

            def graph_output(t, s):
                scaled = probs_all[:, s, 0:GF]
                dve.wait_ge(scale_step[s], t * 3 + 2 + FULL)
                dve.wait_ge(out_rows_psum[s], t + FULL)
                dve.tensor_tensor(scaled.rearrange("p (h d) -> p h d", d=DK),
                                  psum[s][:, 2, :].rearrange("p (h d) -> p h d", d=DK),
                                  total[s][:].unsqueeze(2).to_broadcast([P, GB * GH, DK]), ALU.mult) \
                   .then_inc(scaled_ready[s], 1)
                dve.wait_ge(scaled_ready[s], t + FULL)
                dve.wait_ge(kept[s], t * 16 + 16)
                dve.wait_ge(x_done[s], ATTN_ITS + t + FREED)
                dve.scalar_tensor_tensor(y_sum[s][:], scaled, 0.0, x_keep[s][:], ALU.max, ALU.add) \
                   .then_inc(y_ready[s], 1)

            def graph(now, nxt):
                for s, other, ending in ((0, 1, now), (1, 0, nxt)):
                    if now is not None:
                        gt0(now, s, 1)
                    if nxt is not None:
                        split_lo(ATTN_ITS + nxt, s, 3)
                    if now is not None:
                        output_scale(now, s)
                    if ending is not None:
                        gate(ending, other, 0, 0)
                        gate(ending, other, 0, 1)
                    if now is not None:
                        graph_output(now, s)
                    if nxt is not None:
                        norm_guard(nxt, s)
                        graph_k_lo(nxt, s)
                        normalised(nxt, s)
                    if ending is not None:
                        gt0(ending, other, 0)
                    if nxt is not None:
                        n_lo(nxt, s)
                        graph_q_lo(nxt, s)
                    if ending is not None:
                        graph_maxima(ending, other, 1, 0)
                        first_half(ending, other)
                        graph_maxima(ending, other, 1, 1)
                    if now is not None:
                        statistics(ATTN_ITS + now, s)
                    if ending is not None:
                        gate(ending, other, 1, 0)
                    if nxt is not None:
                        graph_v(nxt, s)
                        graph_maxima(nxt, s, 0, 0)
                    if ending is not None:
                        gate(ending, other, 1, 1)
                    if nxt is not None:
                        graph_maxima(nxt, s, 0, 1)

            dve.memset(eps_col[:], LN_EPS).then_inc(start_ready, 1)
            for s in range(STREAMS):
                dve.memset(pair_diag[s][:].rearrange("p r w c b j -> p (r w c b j)").bitcast(F32), 0.0) \
                   .then_inc(start_ready, 1)
            split_qkv(0)
            split_out(0)
            attention(None, None, 0)
            attention(None, 0, 1)
            with dve.Fori(0, LAYERS - 1) as layer:
                first, after = layer * NT, layer * NT + NT
                with dve.Fori(1, NT - 1) as t:
                    attention(first + t - 1, first + t, first + t + 1)
                split_qkv(layer + 1)
                attention(after - 2, after - 1, after)
                split_out(layer + 1)
                attention(after - 1, after, after + 1)
            first = (LAYERS - 1) * NT
            with dve.Fori(1, NT - 1) as t:
                attention(first + t - 1, first + t, first + t + 1)
            attention(ATTN_ITS - 2, ATTN_ITS - 1, None)
            statistics(ATTN_ITS - 1, 1)

            dve.wait_ge(graph_raw_loaded, 16 * 7)
            for c in range(DC):
                last = dve.tensor_copy(gb_wide[:, c, :], cols[:, 3, c:c + 1].to_broadcast([P, P]))
            last.then_inc(gb_wide_ready, 1)
            for s in range(STREAMS):
                dve.wait_ge(x_keep_ready[s], ATTN_ITS + FREED)
            split_fused()
            graph(None, 0)
            with dve.Fori(0, NT - 1) as t:
                graph(t, t + 1)
            graph(NT - 1, None)


def kernel(x, adj, **w):
    import numpy as np
    import concourse.bacc as bacc
    from concourse.bass_utils import run_bass_kernel_spmd

    def arr(name):
        return np.asarray(w[name])

    x = np.ascontiguousarray(np.asarray(x))
    D = x.shape[2]
    P = 128
    attn = range(3)
    arrays = {
        "x": x,
        "adj": np.ascontiguousarray(np.asarray(adj)).view(np.int32),
        "attn_w": np.stack([np.stack([arr(f"L{l}_gnn_{m}") for m in ("Wq", "Wk", "Wv", "Wo")]) for l in attn]),
        "attn_bo": np.ascontiguousarray(np.broadcast_to(np.stack([arr(f"L{l}_gnn_bo") for l in attn])[:, None], (3, P, D))),
        "gcn_w": np.stack([arr("L3_gnn_map_w").T, arr("L3_gnn_map_w"), arr("L3_gnn_q_w").T, arr("L3_gnn_k_w").T,
                           arr("L3_gnn_gcn_map_w")]),
        "gcn_cols": np.ascontiguousarray(np.stack([arr(f"L3_gnn_{b}") for b in ("map_b", "q_b", "k_b", "gcn_map_b")])
                                         .reshape(4, D // P, P).transpose(2, 0, 1)),
        "gcn_tail": np.ascontiguousarray(arr("L3_gnn_gcn_W").T),
    }
    nc = bacc.Bacc("TRN2", target_bir_lowering=False, num_devices=1)
    args = [nc.dram_tensor(f"in_{n}", a.shape, mybir.dt.from_np(a.dtype), kind="ExternalInput").ap()
            for n, a in arrays.items()]
    out = nc.dram_tensor("out", x.shape, F32, kind="ExternalOutput").ap()
    build(nc, *args, out)
    r = run_bass_kernel_spmd(nc, [{f"in_{n}": a for n, a in arrays.items()}], core_ids=[0])
    return r.results[0]["out"]
```
